# Optimizing a Trainium2 kernel written in Bass

```python
import numpy as np
import jax
import jax.numpy as jnp

def _softmax(x, axis=-1):
    return jax.nn.softmax(x, axis=axis)

def _gelu(x):
    return jax.nn.gelu(x, approximate=True)

def _silu(x):
    return jax.nn.silu(x)

def _sigmoid(x):
    return jax.nn.sigmoid(x)

def _layernorm(x, axis=-1, eps=1e-05):
    m = jnp.mean(x, axis=axis, keepdims=True)
    v = jnp.var(x, axis=axis, keepdims=True)
    return (x - m) / jnp.sqrt(v + eps)

def _scatter_add(tgt, idx, src, axis=0):
    return tgt.at[idx].add(src)

def _segment_sum(src, seg, n):
    return jax.ops.segment_sum(src, seg, n)
kernel_name = 'mk_adj_preln_d1_adj_r2_3c8eb3'

def setup_inputs(seed: int=0):
    np.random.seed(seed)
    _w = jnp.asarray

    def _rec_inputs():
        import jax
        import jax.numpy as jnp
        _gk = jax.random.key(seed)
        x = 7.22e-05 + 1 * jax.random.normal(jax.random.fold_in(_gk, 1), (32, 256, 256), jnp.float32)
        _a = jax.random.bernoulli(jax.random.fold_in(_gk, 2), 0.015625, (256, 256))
        _a = jnp.logical_or(_a, jnp.swapaxes(_a, -1, -2))
        _a = jnp.logical_or(_a, jnp.eye(256, dtype=bool))
        _af = _a.astype(jnp.float32)
        _af = _af * jax.random.uniform(jax.random.fold_in(_gk, 3), (256, 256), jnp.float32, 0.05, 0.00390622)
        adj = _af
        return (x, adj)
    x, adj = _rec_inputs()

    def _L0_gnn_setup():
        import jax, jax.numpy as jnp
        import numpy as np
        B, N, D, T = (64, 128, 256, 3)

        def _lin(v, W, b):
            return jnp.einsum('...i,oi->...o', v, W) + b
        key = jax.random.key(seed)
        ks = jax.random.split(key, 12)
        s2 = 1.0 / np.sqrt(2 * D)
        s1 = 1.0 / np.sqrt(D)
        return {'x': jax.random.normal(ks[0], (B, N, D), jnp.float32), 'in_mat': jax.random.uniform(ks[1], (N, N), jnp.float32) / N, 'out_mat': jax.random.uniform(ks[2], (N, N), jnp.float32) / N, 'w3_w': jax.random.normal(ks[3], (D, 2 * D), jnp.float32) * s2, 'w3_b': jnp.zeros((D,), jnp.float32), 'u3_w': jax.random.normal(ks[4], (D, D), jnp.float32) * s1, 'u3_b': jnp.zeros((D,), jnp.float32), 'w4_w': jax.random.normal(ks[5], (D, 2 * D), jnp.float32) * s2, 'w4_b': jnp.zeros((D,), jnp.float32), 'w5_w': jax.random.normal(ks[6], (D, 2 * D), jnp.float32) * s2, 'w5_b': jnp.zeros((D,), jnp.float32), 'u5_w': jax.random.normal(ks[7], (D, D), jnp.float32) * s1, 'u5_b': jnp.zeros((D,), jnp.float32)}
    _L0_gnn_all = _L0_gnn_setup()
    _L0_gnn_in = {k: v for k, v in _L0_gnn_all.items() if k in ('w3_w', 'w3_b', 'u3_w', 'u3_b', 'w4_w', 'w4_b', 'w5_w', 'w5_b', 'u5_w', 'u5_b')}
    del _L0_gnn_all
    return {'x': x, 'adj': adj, 'L0_gnn_w3_w': _L0_gnn_in['w3_w'], 'L0_gnn_w3_b': _L0_gnn_in['w3_b'], 'L0_gnn_u3_w': _L0_gnn_in['u3_w'], 'L0_gnn_u3_b': _L0_gnn_in['u3_b'], 'L0_gnn_w4_w': _L0_gnn_in['w4_w'], 'L0_gnn_w4_b': _L0_gnn_in['w4_b'], 'L0_gnn_w5_w': _L0_gnn_in['w5_w'], 'L0_gnn_w5_b': _L0_gnn_in['w5_b'], 'L0_gnn_u5_w': _L0_gnn_in['u5_w'], 'L0_gnn_u5_b': _L0_gnn_in['u5_b']}

def reference(x, adj, L0_gnn_w3_w, L0_gnn_w3_b, L0_gnn_u3_w, L0_gnn_u3_b, L0_gnn_w4_w, L0_gnn_w4_b, L0_gnn_w5_w, L0_gnn_w5_b, L0_gnn_u5_w, L0_gnn_u5_b):
    import jax
    import jax.numpy as jnp

    def _L0_gnn_ref(x, in_mat, out_mat, w3_w, w3_b, u3_w, u3_b, w4_w, w4_b, w5_w, w5_b, u5_w, u5_b):
        import jax, jax.numpy as jnp
        import numpy as np
        B, N, D, T = (64, 128, 256, 3)

        def _lin(v, W, b):
            return jnp.einsum('...i,oi->...o', v, W) + b
        h = x
        for _ in range(T):
            a_in = jnp.einsum('nm,bmd->bnd', in_mat, h)
            a_out = jnp.einsum('nm,bmd->bnd', out_mat, h)
            av = jnp.concatenate([a_in, a_out], axis=-1)
            z = jax.nn.sigmoid(_lin(av, w3_w, w3_b) + _lin(h, u3_w, u3_b))
            r = jax.nn.sigmoid(_lin(av, w4_w, w4_b) + _lin(h, u3_w, u3_b))
            hv = jnp.tanh(_lin(av, w5_w, w5_b) + _lin(r * h, u5_w, u5_b))
            h = (1.0 - z) * h + z * hv
        return h
    h = jnp.maximum(_layernorm(x, axis=-1), 0.0)
    x = x + _L0_gnn_ref(h, adj, adj, L0_gnn_w3_w, L0_gnn_w3_b, L0_gnn_u3_w, L0_gnn_u3_b, L0_gnn_w4_w, L0_gnn_w4_b, L0_gnn_w5_w, L0_gnn_w5_b, L0_gnn_u5_w, L0_gnn_u5_b)
    return x

_drawn_inputs = setup_inputs


def setup_inputs(seed=0):
    import zlib

    import numpy as np

    out = dict(_drawn_inputs(seed))
    spreads = {'L0_gnn_w3_b': (0.0, 0.586),
     'L0_gnn_u3_b': (0.0, 0.511),
     'L0_gnn_w4_b': (0.0, 0.8),
     'L0_gnn_w5_b': (0.0, 0.1),
     'L0_gnn_u5_b': (0.0, 0.1)}
    factors = {'L0_gnn_w4_w': 6.146}
    for name, (base, spread) in spreads.items():
        noise = np.random.default_rng([zlib.crc32(name.encode()), seed]).standard_normal(out[name].shape)
        drawn = base * np.exp(spread * noise) if base else spread * noise
        out[name] = jnp.asarray(drawn.astype(out[name].dtype))
    for name, factor in factors.items():
        out[name] = (out[name] * factor).astype(out[name].dtype)
    return out
```

```python
from contextlib import ExitStack

import concourse.bass as bass
from concourse import mybir

F32 = mybir.dt.float32
F32R = mybir.dt.float32r
ALU = mybir.AluOpType
ACT = mybir.ActivationFunctionType

P = 128
EPS = 1e-5

ADJ, U3, W4, W5, W34, U5 = range(6)


def gnn_kernel(nc, x, adj, w3_w, w3_b, u3_w, u3_b, w4_w, w4_b, w5_w, w5_b, u5_w, u5_b, out):
    NBATCH, N, D = x.shape
    STEPS = 3
    GB = 512 // N
    ROWS = GB * N
    KC = D // P
    NCH = N // P
    RB = GB * NCH
    GROUPS = NBATCH // GB
    PAIRS = GROUPS // 2
    SEGS = 2 * STEPS
    LAST = PAIRS * SEGS - 1
    assert D == 256 and N == 256 and GROUPS % 2 == 0

    x_rows = x.rearrange("(g b) (p c) d -> g p b (c d)", b=GB, c=NCH)
    out_rows = out.rearrange("(g b) (p c) d -> g p b (c d)", b=GB, c=NCH)

    with ExitStack() as ctx:
        def sb(name, shape, dt=F32):
            return ctx.enter_context(nc.sbuf_tensor(name, shape, dt))

        def psum(name, shape):
            return ctx.enter_context(nc.psum_tensor(name, shape, F32))

        def sem(name):
            return ctx.enter_context(nc.semaphore(name))

        ident = sb("ident", [P, P])
        neg_half = sb("neg_half", [P, RB])
        w_nat = {k: sb(f"{k}_nat", [P, KC, 2 * D]) for k in ("w3", "w4", "w5")}
        u_nat = {k: sb(f"{k}_nat", [P, KC, D]) for k in ("u3", "u5")}
        adj_nat = sb("adj_nat", [P, NCH, N])
        w_sum = {k: sb(f"{k}_sum", [P, KC, D]) for k in ("w3", "w4", "w5")}
        w_diff = sb("w_diff", [P, KC, D])
        mat_hi = sb("mat_hi", [P, 6, KC, D], F32R)
        mat_lo = sb("mat_lo", [P, 6, KC, D], F32R)
        bias_rows = sb("bias_rows", [5 * KC, P])
        bias_cols = sb("bias_cols", [P, 5 * KC])
        bias_z = sb("bias_z", [P, KC])
        bias_r = sb("bias_r", [P, KC])
        bias_h = sb("bias_h", [P, KC])
        x_in = [sb(f"x_in{q}", [P, RB, D]) for q in range(2)]
        x_keep = [sb(f"x_keep{q}", [P, RB, D]) for q in range(2)]
        h0 = [sb(f"h0_{q}", [P, RB, D]) for q in range(2)]
        nat_hi = [sb(f"nat_hi{q}", [P, RB, D], F32R) for q in range(2)]
        nat_lo = [sb(f"nat_lo{q}", [P, RB, D], F32R) for q in range(2)]
        hT = [sb(f"hT{q}", [P, KC, ROWS]) for q in range(2)]
        hT_hi = [sb(f"hT_hi{q}", [P, KC, ROWS], F32R) for q in range(2)]
        hT_lo = [sb(f"hT_lo{q}", [P, KC, ROWS], F32R) for q in range(2)]
        y_out = [sb(f"y_out{q}", [P, RB, D]) for q in range(2)]
        a_hi = sb("a_hi", [P, KC, ROWS], F32R)
        a_lo = sb("a_lo", [P, KC, ROWS], F32R)
        r = sb("r", [P, KC, ROWS])
        rh = sb("rh", [P, KC, ROWS])
        rh_hi = sb("rh_hi", [P, KC, ROWS], F32R)
        rh_lo = sb("rh_lo", [P, KC, ROWS], F32R)
        z = sb("z", [P, KC, ROWS])
        hv = sb("hv", [P, KC, ROWS])
        delta = sb("delta", [P, KC, ROWS])
        stats = sb("stats", [P, RB, 6])
        mean2 = sb("mean2", [P, RB])
        mdiff = sb("mdiff", [P, RB])
        msq = sb("msq", [P, RB])
        m2sum = sb("m2sum", [P, RB])
        mean = sb("mean", [P, RB])
        var = sb("var", [P, RB])
        rstd = sb("rstd", [P, RB])

        ps_a = psum("ps_a", [P, KC, ROWS])
        ps_r = psum("ps_r", [P, KC, ROWS])
        ps_h = psum("ps_h", [P, KC, ROWS])
        ps_t = psum("ps_t", [P, 2, ROWS])

        w_loaded = sem("w_loaded")
        b_loaded = sem("b_loaded")
        x_loaded = [sem("x_loaded_a"), sem("x_loaded_b")]
        y_free = [sem("y_free_a"), sem("y_free_b")]
        ident_zero = sem("ident_zero")
        ident_ready = sem("ident_ready")
        w_summed = sem("w_summed")
        mat_turned = sem("mat_turned")
        mat_hi_ready = sem("mat_hi_ready")
        mat_ready = sem("mat_ready")
        bias_turned = sem("bias_turned")
        bias_copied = sem("bias_copied")
        bias_ready = sem("bias_ready")
        agg_done = sem("agg_done")
        r_pre_done = sem("r_pre_done")
        z_pre_done = sem("z_pre_done")
        hv_pre_done = sem("hv_pre_done")
        a_hi_ready = sem("a_hi_ready")
        a_split = sem("a_split")
        r_ready = sem("r_ready")
        z_ready = sem("z_ready")
        hv_ready = sem("hv_ready")
        rh_ready = sem("rh_ready")
        rh_hi_ready = sem("rh_hi_ready")
        rh_split = sem("rh_split")
        delta_ready = sem("delta_ready")
        zdelta_ready = sem("zdelta_ready")
        hT_new = sem("hT_new")
        hT_hi_ready = sem("hT_hi_ready")
        hT_split = sem("hT_split")
        nat_hi_ready = sem("nat_hi_ready")
        turned = sem("turned")
        turn_taken = sem("turn_taken")
        stat_step = sem("stat_step")
        rstd_ready = sem("rstd_ready")
        centred = sem("centred")
        h0_ready = sem("h0_ready")
        nat0_split = sem("nat0_split")
        x_kept = [sem("x_kept_a"), sem("x_kept_b")]

        def seg(pair, j):
            return pair * SEGS + j

        TURNS = SEGS + 2

        def turns_before(pair, j):
            return pair * TURNS + (j + 1 if j else 0)

        def sum_taken(pair, q):
            if q == 0:
                return 2 * (turns_before(pair, SEGS - 1) + 1)
            return 2 * (turns_before(pair + 1, 0) + 1)

        ALL_TAKEN = 2 * PAIRS * TURNS
        STAT_STEPS = 6

        def triple(pe, dst, st_hi, st_lo, mv_hi, mv_lo, first, last):
            pe.matmul(dst, st_hi, mv_hi, start=first, stop=False, skip_group_check=True)
            pe.matmul(dst, st_hi, mv_lo, start=False, stop=False, skip_group_check=True)
            return pe.matmul(dst, st_lo, mv_hi, start=False, stop=last, skip_group_check=True)

        def product(pe, dst, mat, o, mv_hi, mv_lo, k, first, last):
            cols = slice(o * P, (o + 1) * P)
            return triple(pe, dst[:, o, :], mat_hi[:, mat, k, cols], mat_lo[:, mat, k, cols],
                          mv_hi[:, k, :], mv_lo[:, k, :], first, last)

        def mat_bank(i):
            return (ps_a, ps_r, ps_h)[i // 2][:, i % 2, :].rearrange("p (k o) -> p k o", k=KC)

        def bits(t):
            return t.bitcast(F32)

        block = ctx.enter_context(nc.Block())

        @block.sync
        def _(sp):
            def batches(t):
                return t[:].rearrange("p (b c) d -> p b (c d)", b=GB)

            for q in range(2):
                sp.sem_inc(y_free[q], 16)
            sp.dma_start(batches(x_in[0]), x_rows[0]).then_inc(x_loaded[0], 16)
            for w, t in ((w4_w, w_nat["w4"]), (w5_w, w_nat["w5"]), (w3_w, w_nat["w3"]),
                         (u3_w, u_nat["u3"]), (u5_w, u_nat["u5"])):
                sp.dma_start(t[:], w.rearrange("(c p) d -> p c d", p=P)).then_inc(w_loaded, 16)
            sp.dma_start(adj_nat[:], adj.rearrange("(p c) m -> p c m", c=NCH)).then_inc(w_loaded, 16)
            for i, b in enumerate((w3_b, u3_b, w4_b, w5_b, u5_b)):
                sp.dma_start(bias_rows[i * KC:(i + 1) * KC, :], b.rearrange("(c p) -> c p", p=P)).then_inc(b_loaded, 16)
            sp.dma_start(batches(x_in[1]), x_rows[1]).then_inc(x_loaded[1], 16)

            def load_next(pair, q):
                sp.wait_ge(x_kept[q], pair + 1)
                sp.dma_start(batches(x_in[q]), x_rows[2 * (pair + 1) + q]).then_inc(x_loaded[q], 16)

            def store(pair, q, taken):
                sp.wait_ge(turn_taken, taken)
                sp.dma_start(out_rows[2 * pair + q], batches(y_out[q])).then_inc(y_free[q], 16)

            with sp.Fori(0, PAIRS - 1) as pair:
                for q in range(2):
                    load_next(pair, q)
                for q in range(2):
                    store(pair, q, sum_taken(pair, q))
            store(PAIRS - 1, 0, sum_taken(PAIRS - 1, 0))
            store(PAIRS - 1, 1, ALL_TAKEN)
            for q in range(2):
                sp.wait_ge(y_free[q], 16 * (PAIRS + 1))

        @block.gpsimd
        def _(pool):
            nc.gpsimd.memset(ident[:], 0.0).then_inc(ident_zero, 1)
            pool.wait_ge(ident_zero, 1)
            nc.gpsimd.affine_select(out=ident[:], in_=ident[:], compare_op=ALU.not_equal, fill=1.0, base=0,
                                    pattern=[[-1, P]], channel_multiplier=1).then_inc(ident_ready, 1)
            nc.gpsimd.memset(neg_half[:], -0.5).then_inc(ident_ready, 1)
            pool.wait_ge(ident_ready, 2)
            with pool.Fori(0, GROUPS) as group:
                pool.wait_ge(stat_step, group * STAT_STEPS + STAT_STEPS)
                nc.gpsimd.tensor_tensor(rstd[:], var[:], neg_half[:], ALU.pow).then_inc(rstd_ready, 1)

        @block.tensor
        def _(pe):
            def turn_matrix(i, rows):
                for k in range(KC):
                    for o in range(KC):
                        t = pe.transpose(mat_bank(i)[:, k, o * P:(o + 1) * P], rows(o, k), ident[:])
                t.then_inc(mat_turned, 1)

            def turn_new(group, q):
                pe.wait_ge(h0_ready, group + 1)
                for k in range(KC):
                    for b in range(RB):
                        t = pe.transpose(ps_t[:, k, b * P:(b + 1) * P], h0[q][:, b, k * P:(k + 1) * P], ident[:])
                    t.then_inc(turned, 1)

            def turn_state(s, q, taken):
                pe.wait_ge(turn_taken, taken)
                pe.wait_ge(hT_new, 2 * s + 2)
                for b in range(RB):
                    for k in range(KC):
                        at = (b % 2) * D + k * P
                        t = pe.transpose(ps_t[:, b // 2, at:at + P], hT[q][:, k, b * P:(b + 1) * P], ident[:])
                    if b % 2 == 1:
                        t.then_inc(turned, 1)

            def segment(pair, j, tail=True, new=False):
                s, q = seg(pair, j), j % 2
                if j < 2:
                    pe.wait_ge(nat0_split, 2 * pair + q + 1)
                else:
                    pe.wait_ge(turn_taken, 2 * turns_before(pair, j))
                if tail:
                    pe.wait_ge(a_split, 2 * s)
                for c in range(KC):
                    cols = slice(c * P, (c + 1) * P)
                    for b in range(GB):
                        for m in range(NCH):
                            mm = triple(pe, ps_a[:, c, b * N:(b + 1) * N],
                                        nat_hi[q][:, b * NCH + m, cols], nat_lo[q][:, b * NCH + m, cols],
                                        mat_hi[:, ADJ, m, :], mat_lo[:, ADJ, m, :], m == 0, m == NCH - 1)
                    mm.then_inc(agg_done, 1)
                pe.wait_ge(hT_split, 2 * s + 2)
                if tail:
                    pe.wait_ge(z_ready, 2 * s)
                for o in range(KC):
                    for k in range(KC):
                        product(pe, ps_r, U3, o, hT_hi[q], hT_lo[q], k, k == 0, False)
                for o in range(KC):
                    for k in range(KC):
                        if o == 0:
                            pe.wait_ge(a_split, 2 * s + k + 1)
                        mm = product(pe, ps_r, W4, o, a_hi, a_lo, k, False, k == KC - 1)
                    mm.then_inc(r_pre_done, 1)
                if tail:
                    turn_state(s - 1, 1 - q, 2 * turns_before(pair, j))
                    pe.wait_ge(hv_ready, 2 * s)
                for o in range(KC):
                    for k in range(KC):
                        product(pe, ps_h, W5, o, a_hi, a_lo, k, k == 0, False)
                for o in range(KC):
                    pe.wait_ge(r_ready, 2 * s + o + 1)
                    for k in range(KC):
                        mm = product(pe, ps_r, W34, o, a_hi, a_lo, k, False, k == KC - 1)
                    mm.then_inc(z_pre_done, 1)
                if new:
                    pe.wait_ge(turn_taken, 2 * (turns_before(pair, j) + 1))
                    turn_new(2 * pair + 1 if j == 0 else 2 * pair + 2, 1 - q)
                for o in range(KC):
                    for k in range(KC):
                        if o == 0:
                            pe.wait_ge(rh_split, 2 * s + k + 1)
                        mm = product(pe, ps_h, U5, o, rh_hi, rh_lo, k, False, k == KC - 1)
                    mm.then_inc(hv_pre_done, 1)

            pe.wait_ge(ident_ready, 1)
            pe.wait_ge(b_loaded, 5 * 16)
            pe.transpose(ps_t[:, 0, 0:5 * KC], bias_rows[:], ident[0:5 * KC, 0:5 * KC]).then_inc(bias_turned, 1)
            pe.wait_ge(w_loaded, 6 * 16)
            turn_matrix(ADJ, lambda o, k: adj_nat[:, o, k:N:NCH])
            turn_matrix(U3, lambda o, k: u_nat["u3"][:, o, k * P:(k + 1) * P])
            pe.wait_ge(w_summed, 1)
            turn_matrix(W4, lambda o, k: w_sum["w4"][:, o, k * P:(k + 1) * P])
            pe.wait_ge(w_summed, 2)
            turn_matrix(W5, lambda o, k: w_sum["w5"][:, o, k * P:(k + 1) * P])
            pe.wait_ge(w_summed, 4)
            turn_matrix(W34, lambda o, k: w_diff[:, o, k * P:(k + 1) * P])
            turn_matrix(U5, lambda o, k: u_nat["u5"][:, o, k * P:(k + 1) * P])
            pe.wait_ge(bias_copied, 1)
            turn_new(0, 0)
            pe.wait_ge(mat_ready, 6)

            segment(0, 0, tail=False, new=True)
            with pe.Fori(0, PAIRS - 1) as pair:
                for j in range(1, SEGS):
                    segment(pair, j, new=j == SEGS - 1)
                segment(pair + 1, 0, new=True)
            for j in range(1, SEGS):
                segment(PAIRS - 1, j)
            turn_state(LAST, 1, ALL_TAKEN - 2)

        @block.scalar
        def _(act):
            def split_new(group, q):
                act.wait_ge(h0_ready, group + 1)
                nc.scalar.activation(nat_hi[q][:], h0[q][:], ACT.Copy).then_inc(nat_hi_ready, 2)

            def take_new(q, turn):
                for k in range(KC):
                    act.wait_ge(turned, 2 * turn + k + 1)
                    nc.scalar.activation(hT_hi[q][:, k, :], ps_t[:, k, :], ACT.Copy).then_inc(hT_hi_ready, 1)
                    nc.scalar.activation(hT[q][:, k, :], ps_t[:, k, :], ACT.Copy).then_inc(turn_taken, 1)

            def keep_x(pair, q, taken):
                act.wait_ge(turn_taken, taken)
                act.wait_ge(h0_ready, 2 * pair + q + 1)
                act.wait_ge(x_loaded[q], 16 * (pair + 1))
                nc.scalar.activation(x_keep[q][:], x_in[q][:], ACT.Copy).then_inc(x_kept[q], 1)

            def segment(pair, j, tail=True, new=False, more=True):
                s, q = seg(pair, j), j % 2
                last_step = j in (0, SEGS - 1)
                if j in (2, 3):
                    keep_x(pair, q, 2 * turns_before(pair, j))
                for c in range(KC):
                    act.wait_ge(agg_done, 2 * s + c + 1)
                    nc.scalar.activation(a_hi[:, c, :], ps_a[:, c, :], ACT.Copy).then_inc(a_hi_ready, 1)
                if tail and not last_step:
                    for c in range(KC):
                        act.wait_ge(hT_new, 2 * s - 1 + c)
                        nc.scalar.activation(hT_hi[1 - q][:, c, :], hT[1 - q][:, c, :],
                                             ACT.Copy).then_inc(hT_hi_ready, 1)
                if tail:
                    act.wait_ge(rh_ready, 2 * s)
                for o in range(KC):
                    act.wait_ge(r_pre_done, 2 * s + o + 1)
                    nc.scalar.activation(r[:, o, :], ps_r[:, o, :], ACT.Sigmoid,
                                         bias=bias_r[:, o:o + 1]).then_inc(r_ready, 1)
                if tail and not last_step:
                    for b in range(2):
                        act.wait_ge(turned, 2 * turns_before(pair, j) + b + 1)
                        nc.scalar.activation(nat_hi[1 - q][:, 2 * b:2 * b + 2, :], ps_t[:, b, :],
                                             ACT.Copy).then_inc(nat_hi_ready, 1)
                if j >= SEGS - 2 and more:
                    split_new(2 * (pair + 1) + q, q)
                if tail:
                    act.wait_ge(zdelta_ready, 2 * s)
                for o in range(KC):
                    act.wait_ge(z_pre_done, 2 * s + o + 1)
                    nc.scalar.activation(z[:, o, :], ps_r[:, o, :], ACT.Sigmoid,
                                         bias=bias_z[:, o:o + 1]).then_inc(z_ready, 1)
                if new:
                    take_new(1 - q, turns_before(pair, j) + 1)
                for o in range(KC):
                    act.wait_ge(hv_pre_done, 2 * s + o + 1)
                    nc.scalar.activation(hv[:, o, :], ps_h[:, o, :], ACT.Tanh,
                                         bias=bias_h[:, o:o + 1]).then_inc(hv_ready, 1)

            for i in range(6):
                act.wait_ge(mat_turned, i + 1)
                nc.scalar.activation(mat_hi[:, i], mat_bank(i), ACT.Copy).then_inc(mat_hi_ready, 1)
            split_new(0, 0)
            take_new(0, 0)
            split_new(1, 1)
            act.wait_ge(bias_ready, 3)
            segment(0, 0, tail=False, new=True)
            with act.Fori(0, PAIRS - 1) as pair:
                for j in range(1, SEGS):
                    segment(pair, j, new=j == SEGS - 1)
                segment(pair + 1, 0, new=True)
            for j in range(1, SEGS):
                segment(PAIRS - 1, j, more=False)

        @block.vector
        def _(dve):
            def measure(group, pair, q):
                step = lambda n: group * STAT_STEPS + n
                dve.wait_ge(x_loaded[q], 16 * (pair + 1))
                for b in range(RB):
                    last = nc.vector.bn_stats(stats[:, b, :], x_in[q][:, b, :])
                last.then_inc(stat_step, 1)
                dve.wait_ge(stat_step, step(1))
                nc.vector.tensor_tensor(mean2[:], stats[:, :, 1], stats[:, :, 4], ALU.add)
                nc.vector.tensor_tensor(mdiff[:], stats[:, :, 1], stats[:, :, 4], ALU.subtract)
                nc.vector.tensor_tensor(m2sum[:], stats[:, :, 2], stats[:, :, 5], ALU.add).then_inc(stat_step, 1)
                dve.wait_ge(stat_step, step(2))
                nc.vector.tensor_tensor(msq[:], mdiff[:], mdiff[:], ALU.mult).then_inc(stat_step, 1)
                nc.vector.tensor_scalar(mean[:], mean2[:], 0.5, None, ALU.mult).then_inc(stat_step, 1)
                dve.wait_ge(stat_step, step(4))
                nc.vector.tensor_scalar(msq[:], msq[:], 0.25, EPS, ALU.mult, ALU.add).then_inc(stat_step, 1)
                dve.wait_ge(stat_step, step(5))
                nc.vector.scalar_tensor_tensor(out=var[:], in0=m2sum[:], scalar=1.0 / D, in1=msq[:],
                                               op0=ALU.mult, op1=ALU.add).then_inc(stat_step, 1)

            def normalise(group, q):
                dve.wait_ge(rstd_ready, group + 1)
                for b in range(RB):
                    last = nc.vector.tensor_scalar(h0[q][:, b, :], x_in[q][:, b, :], mean[:, b:b + 1],
                                                   rstd[:, b:b + 1], ALU.subtract, ALU.mult)
                last.then_inc(centred, 1)
                dve.wait_ge(centred, group + 1)
                nc.vector.tensor_scalar(h0[q][:], h0[q][:], 0.0, None, ALU.max).then_inc(h0_ready, 1)

            def split_new(group, q, s):
                dve.wait_ge(nat_hi_ready, 2 * s + 2)
                nc.vector.tensor_tensor(nat_lo[q][:], h0[q][:], bits(nat_hi[q][:]),
                                        ALU.subtract).then_inc(nat0_split, 1)

            def take_new(q, s, turn):
                for k in range(KC):
                    dve.wait_ge(hT_hi_ready, 2 * s + k + 1)
                    dve.wait_ge(turn_taken, 2 * turn + k + 1)
                    nc.vector.tensor_tensor(hT_lo[q][:, k, :], hT[q][:, k, :], bits(hT_hi[q][:, k, :]),
                                            ALU.subtract).then_inc(hT_split, 1)

            def make_delta(s, q, c):
                dve.wait_ge(hv_ready, 2 * s + c + 1)
                nc.vector.tensor_tensor(delta[:, c, :], hv[:, c, :], hT[q][:, c, :],
                                        ALU.subtract).then_inc(delta_ready, 1)

            def make_zdelta(s, c):
                dve.wait_ge(delta_ready, 2 * s + c + 1)
                nc.vector.tensor_tensor(delta[:, c, :], z[:, c, :], delta[:, c, :],
                                        ALU.mult).then_inc(zdelta_ready, 1)

            def make_state(s, q, c):
                dve.wait_ge(zdelta_ready, 2 * s + c + 1)
                nc.vector.tensor_tensor(hT[q][:, c, :], hT[q][:, c, :], delta[:, c, :],
                                        ALU.add).then_inc(hT_new, 1)

            def split_a(s, c):
                dve.wait_ge(a_hi_ready, 2 * s + c + 1)
                nc.vector.tensor_tensor(a_lo[:, c, :], ps_a[:, c, :], bits(a_hi[:, c, :]),
                                        ALU.subtract).then_inc(a_split, 1)

            def split_state(s, q):
                for c in range(KC):
                    dve.wait_ge(hT_hi_ready, 2 * s + c + 1)
                    nc.vector.tensor_tensor(hT_lo[q][:, c, :], hT[q][:, c, :], bits(hT_hi[q][:, c, :]),
                                            ALU.subtract).then_inc(hT_split, 1)

            def take_state(s, q, turn):
                for b in range(2):
                    dve.wait_ge(nat_hi_ready, 2 * s + b + 1)
                    nc.vector.tensor_tensor(nat_lo[q][:, 2 * b:2 * b + 2, :], ps_t[:, b, :].rearrange("p (b d) -> p b d", b=2),
                                            bits(nat_hi[q][:, 2 * b:2 * b + 2, :]),
                                            ALU.subtract).then_inc(turn_taken, 1)

            def add_x(pair, q, turn):
                dve.wait_ge(y_free[q], 16 * (pair + 1))
                for b in range(2):
                    dve.wait_ge(turned, 2 * turn + b + 1)
                    nc.vector.tensor_tensor(y_out[q][:, 2 * b:2 * b + 2, :],
                                            ps_t[:, b, :].rearrange("p (b d) -> p b d", b=2),
                                            x_keep[q][:, 2 * b:2 * b + 2, :], ALU.add).then_inc(turn_taken, 1)

            def segment(pair, j, tail=True, new=False, more=True):
                s, q = seg(pair, j), j % 2
                last_step = j in (0, SEGS - 1)
                if tail:
                    make_delta(s - 1, 1 - q, 0)
                    make_zdelta(s - 1, 0)
                    make_state(s - 1, 1 - q, 0)
                    split_a(s, 0)
                    make_delta(s - 1, 1 - q, 1)
                    split_a(s, 1)
                    make_zdelta(s - 1, 1)
                    make_state(s - 1, 1 - q, 1)
                else:
                    for c in range(KC):
                        split_a(s, c)
                if tail and not last_step:
                    split_state(s + 1, 1 - q)
                for c in range(KC):
                    dve.wait_ge(r_ready, 2 * s + c + 1)
                    nc.vector.tensor_tensor(rh[:, c, :], r[:, c, :], hT[q][:, c, :], ALU.mult).then_inc(rh_ready, 1)
                    dve.wait_ge(rh_ready, 2 * s + c + 1)
                    nc.vector.tensor_copy(rh_hi[:, c, :], rh[:, c, :]).then_inc(rh_hi_ready, 1)
                    dve.wait_ge(rh_hi_ready, 2 * s + c + 1)
                    nc.vector.tensor_tensor(rh_lo[:, c, :], rh[:, c, :], bits(rh_hi[:, c, :]),
                                            ALU.subtract).then_inc(rh_split, 1)
                if j in (3, 4) and more:
                    measure(2 * (pair + 1) + 1 - q, pair + 1, 1 - q)
                if tail and not last_step:
                    take_state(s + 1, 1 - q, turns_before(pair, j))
                elif tail:
                    add_x(pair if j else pair - 1, 1 - q, turns_before(pair, j))
                if j in (3, 4) and more:
                    normalise(2 * (pair + 1) + 1 - q, 1 - q)
                if j >= SEGS - 2 and more:
                    split_new(2 * (pair + 1) + q, q, seg(pair + 1, q))
                if new:
                    take_new(1 - q, s + 1, turns_before(pair, j) + 1)

            dve.wait_ge(w_loaded, 6 * 16)
            for k in ("w4", "w5", "w3"):
                nc.vector.tensor_tensor(w_sum[k][:], w_nat[k][:, :, 0:D], w_nat[k][:, :, D:2 * D],
                                        ALU.add).then_inc(w_summed, 1)
            dve.wait_ge(w_summed, 3)
            nc.vector.tensor_tensor(w_diff[:], w_sum["w3"][:], w_sum["w4"][:], ALU.subtract).then_inc(w_summed, 1)
            dve.wait_ge(bias_turned, 1)
            nc.vector.tensor_copy(bias_cols[:], ps_t[:, 0, 0:5 * KC]).then_inc(bias_copied, 1)
            dve.wait_ge(bias_copied, 1)
            b_w3, b_u3, b_w4, b_w5, b_u5 = (bias_cols[:, i * KC:(i + 1) * KC] for i in range(5))
            nc.vector.tensor_tensor(bias_z[:], b_w3, b_u3, ALU.add).then_inc(bias_ready, 1)
            nc.vector.tensor_tensor(bias_r[:], b_w4, b_u3, ALU.add).then_inc(bias_ready, 1)
            nc.vector.tensor_tensor(bias_h[:], b_w5, b_u5, ALU.add).then_inc(bias_ready, 1)
            measure(0, 0, 0)
            normalise(0, 0)
            for i in range(6):
                dve.wait_ge(mat_hi_ready, i + 1)
                nc.vector.tensor_tensor(mat_lo[:, i], mat_bank(i), bits(mat_hi[:, i]),
                                        ALU.subtract).then_inc(mat_ready, 1)
            split_new(0, 0, 0)
            take_new(0, 0, 0)
            measure(1, 0, 1)
            normalise(1, 1)
            split_new(1, 1, 1)

            segment(0, 0, tail=False, new=True)
            with dve.Fori(0, PAIRS - 1) as pair:
                for j in range(1, SEGS):
                    segment(pair, j, new=j == SEGS - 1)
                segment(pair + 1, 0, new=True)
            for j in range(1, SEGS):
                segment(PAIRS - 1, j, more=False)
            for c in range(KC):
                make_delta(LAST, 1, c)
                make_zdelta(LAST, c)
                make_state(LAST, 1, c)
            add_x(PAIRS - 1, 1, ALL_TAKEN // 2 - 1)


_INS = ["x", "adj", "L0_gnn_w3_w", "L0_gnn_w3_b", "L0_gnn_u3_w", "L0_gnn_u3_b", "L0_gnn_w4_w", "L0_gnn_w4_b",
        "L0_gnn_w5_w", "L0_gnn_w5_b", "L0_gnn_u5_w", "L0_gnn_u5_b"]


def kernel(**inputs):
    import numpy as _np
    import concourse.bacc as _bacc
    from concourse import mybir as _mybir
    from concourse.bass_utils import run_bass_kernel_spmd as _run

    nc = _bacc.Bacc("TRN2", target_bir_lowering=False, num_devices=1)
    arrays, args = {}, []
    for name in _INS:
        a = _np.ascontiguousarray(inputs[name])
        arrays[f"in_{name}"] = a
        args.append(nc.dram_tensor(f"in_{name}", a.shape, _mybir.dt.from_np(a.dtype), kind="ExternalInput").ap())
    x = inputs["x"]
    args.append(nc.dram_tensor("out_x", x.shape, _mybir.dt.from_np(_np.dtype("float32")), kind="ExternalOutput").ap())
    gnn_kernel(nc, *args)
    r = _run(nc, [arrays], core_ids=[0])
    return r.results[0]["out_x"]
```

```python
from contextlib import ExitStack

import concourse.bass as bass
from concourse import mybir

F32 = mybir.dt.float32
F32R = mybir.dt.float32r
ALU = mybir.AluOpType
ACT = mybir.ActivationFunctionType

P = 128
EPS = 1e-5

ADJ, U3, W4, W5, W34, U5 = range(6)


def gnn_kernel(nc, x, adj, w3_w, w3_b, u3_w, u3_b, w4_w, w4_b, w5_w, w5_b, u5_w, u5_b, out):
    NBATCH, N, D = x.shape
    STEPS = 3
    GB = 512 // N
    ROWS = GB * N
    KC = D // P
    NCH = N // P
    RB = GB * NCH
    GROUPS = NBATCH // GB
    PAIRS = GROUPS // 2
    SEGS = 2 * STEPS
    LAST = PAIRS * SEGS - 1
    BK = 32
    BP = P // BK
    assert D == 256 and N == 256 and GROUPS % 2 == 0

    x_rows = x.rearrange("(g b) (p c) d -> g p b (c d)", b=GB, c=NCH)
    out_rows = out.rearrange("(g b) (p c) d -> g p b (c d)", b=GB, c=NCH)

    with ExitStack() as ctx:
        def sb(name, shape, dt=F32):
            return ctx.enter_context(nc.sbuf_tensor(name, shape, dt))

        def psum(name, shape):
            return ctx.enter_context(nc.psum_tensor(name, shape, F32))

        def sem(name):
            return ctx.enter_context(nc.semaphore(name))

        ident = sb("ident", [P, P])
        neg_half = sb("neg_half", [P, RB])
        warm = sb("warm", [P, 1])
        w_nat = {k: sb(f"{k}_nat", [P, KC, 2 * D]) for k in ("w3", "w4", "w5")}
        u_nat = {k: sb(f"{k}_nat", [P, KC, D]) for k in ("u3", "u5")}
        adj_nat = sb("adj_nat", [P, NCH, N])
        w_sum = {k: sb(f"{k}_sum", [P, KC, D]) for k in ("w3", "w4", "w5")}
        w_diff = sb("w_diff", [P, KC, D])
        mat_hi = sb("mat_hi", [P, 6, KC, D], F32R)
        mat_lo = sb("mat_lo", [P, 6, KC, D], F32R)
        bias_rows = sb("bias_rows", [5 * KC, P])
        bias_cols = sb("bias_cols", [P, 5 * KC])
        bias_z = sb("bias_z", [P, KC])
        bias_r = sb("bias_r", [P, KC])
        bias_h = sb("bias_h", [P, KC])
        x_in = [sb(f"x_in{q}", [P, RB, D]) for q in range(2)]
        x_keep = [sb(f"x_keep{q}", [P, RB, D]) for q in range(2)]
        normed = [sb(f"normed{q}", [P, RB, D]) for q in range(2)]
        nat_hi = [sb(f"nat_hi{q}", [P, RB, D], F32R) for q in range(2)]
        nat_lo = [sb(f"nat_lo{q}", [P, RB, D], F32R) for q in range(2)]
        hT = [sb(f"hT{q}", [P, KC, ROWS]) for q in range(2)]
        hT_hi = [sb(f"hT_hi{q}", [P, KC, ROWS], F32R) for q in range(2)]
        hT_lo = [sb(f"hT_lo{q}", [P, KC, ROWS], F32R) for q in range(2)]
        y_out = [sb(f"y_out{q}", [P, RB, D]) for q in range(2)]
        a_hi = sb("a_hi", [P, KC, ROWS], F32R)
        a_lo = sb("a_lo", [P, KC, ROWS], F32R)
        r = sb("r", [P, KC, ROWS])
        rh = sb("rh", [P, KC, ROWS])
        rh_hi = sb("rh_hi", [P, KC, ROWS], F32R)
        rh_lo = sb("rh_lo", [P, KC, ROWS], F32R)
        z = sb("z", [P, KC, ROWS])
        hv = sb("hv", [P, KC, ROWS])
        delta = sb("delta", [P, KC, ROWS])
        blocks = sb("blocks", [P, BP, KC, RB, BK])
        moved = sb("moved", [P, BP, KC, RB, BK])
        bounce = nc.dram_tensor("bounce", [P, BP, KC * RB * BK], F32, kind="Internal").ap()
        stats = sb("stats", [P, RB, 6])
        mean2 = sb("mean2", [P, RB])
        mdiff = sb("mdiff", [P, RB])
        msq = sb("msq", [P, RB])
        m2sum = sb("m2sum", [P, RB])
        var = sb("var", [P, RB])
        neg_mean = [sb(f"neg_mean{q}", [P, RB]) for q in range(2)]
        rstd = [sb(f"rstd{q}", [P, RB]) for q in range(2)]

        ps_a = psum("ps_a", [P, KC, ROWS])
        ps_r = psum("ps_r", [P, KC, ROWS])
        ps_h = psum("ps_h", [P, KC, ROWS])
        ps_t = psum("ps_t", [P, 2, ROWS])

        loaded = {k: sem(f"{k}_loaded") for k in ("adj", "u3", "w4", "w5", "w3", "u5")}
        b_loaded = sem("b_loaded")
        x_loaded = [sem("x_loaded_a"), sem("x_loaded_b")]
        y_free = [sem("y_free_a"), sem("y_free_b")]
        ident_zero = sem("ident_zero")
        ident_ready = sem("ident_ready")
        w_summed = sem("w_summed")
        mat_turned = sem("mat_turned")
        mat_hi_ready = sem("mat_hi_ready")
        mat_ready = sem("mat_ready")
        bias_turned = sem("bias_turned")
        bias_copied = sem("bias_copied")
        bias_ready = sem("bias_ready")
        tables_in = sem("tables_in")
        agg_done = sem("agg_done")
        r_pre_done = sem("r_pre_done")
        z_pre_done = sem("z_pre_done")
        hv_pre_done = sem("hv_pre_done")
        a_hi_ready = sem("a_hi_ready")
        a_split = sem("a_split")
        r_ready = sem("r_ready")
        z_ready = sem("z_ready")
        hv_ready = sem("hv_ready")
        rh_ready = sem("rh_ready")
        rh_hi_ready = sem("rh_hi_ready")
        rh_split = sem("rh_split")
        delta_ready = sem("delta_ready")
        zdelta_ready = sem("zdelta_ready")
        hT_new = sem("hT_new")
        hT_hi_ready = sem("hT_hi_ready")
        hT_split = sem("hT_split")
        blocks_ready = sem("blocks_ready")
        nat_hi_ready = sem("nat_hi_ready")
        nat_split = sem("nat_split")
        bounced = sem("bounced")
        moved_in = sem("moved_in")
        turned = sem("turned")
        turn_taken = sem("turn_taken")
        stat_step = sem("stat_step")
        rstd_ready = sem("rstd_ready")
        centred = sem("centred")
        normed_ready = sem("normed_ready")
        new_nat_hi_ready = sem("new_nat_hi_ready")
        new_nat_split = sem("new_nat_split")
        y_ready = sem("y_ready")
        x_kept = [sem("x_kept_a"), sem("x_kept_b")]

        def seg(pair, j):
            return pair * SEGS + j

        def moved_before(pair, j):
            return pair * (SEGS - 2) + j - 2

        def new_group(pair, j):
            return 2 * pair + (1 if j == 0 else 2)

        STAT_STEPS = 6

        def triple(pe, dst, st_hi, st_lo, mv_hi, mv_lo, first, last):
            pe.matmul(dst, st_hi, mv_hi, start=first, stop=False, skip_group_check=True)
            pe.matmul(dst, st_hi, mv_lo, start=False, stop=False, skip_group_check=True)
            return pe.matmul(dst, st_lo, mv_hi, start=False, stop=last, skip_group_check=True)

        def product(pe, dst, mat, o, mv_hi, mv_lo, k, first, last):
            cols = slice(o * P, (o + 1) * P)
            return triple(pe, dst[:, o, :], mat_hi[:, mat, k, cols], mat_lo[:, mat, k, cols],
                          mv_hi[:, k, :], mv_lo[:, k, :], first, last)

        def mat_bank(i):
            return (ps_r, ps_h, ps_t)[i // 2][:, i % 2, :].rearrange("p (k o) -> p k o", k=KC)

        def moved_chunk(k):
            return moved[:, :, k].rearrange("p q b f -> p b q f")

        def chunk(t, k):
            return t[:, :, k * P:(k + 1) * P].rearrange("p b (q f) -> p b q f", f=BK)

        def bits(t):
            return t.bitcast(F32)

        block = ctx.enter_context(nc.Block())

        @block.sync
        def _(sp):
            def batches(t):
                return t[:].rearrange("p (b c) d -> p b (c d)", b=GB)

            for q in range(2):
                sp.sem_inc(y_free[q], 16)
            sp.dma_start(batches(x_in[0]), x_rows[0]).then_inc(x_loaded[0], 16)
            sp.dma_start(adj_nat[:], adj.rearrange("(p c) m -> p c m", c=NCH)).then_inc(loaded["adj"], 16)
            for k, w, t in (("u3", u3_w, u_nat["u3"]), ("w4", w4_w, w_nat["w4"]), ("w5", w5_w, w_nat["w5"]),
                            ("w3", w3_w, w_nat["w3"]), ("u5", u5_w, u_nat["u5"])):
                sp.dma_start(t[:], w.rearrange("(c p) d -> p c d", p=P)).then_inc(loaded[k], 16)
            sp.dma_start(batches(x_in[1]), x_rows[1]).then_inc(x_loaded[1], 16)

            def load_next(pair, q):
                sp.wait_ge(x_kept[q], pair + 1)
                sp.dma_start(batches(x_in[q]), x_rows[2 * (pair + 1) + q]).then_inc(x_loaded[q], 16)

            def store(pair, q):
                sp.wait_ge(y_ready, 2 * pair + q + 1)
                sp.dma_start(out_rows[2 * pair + q], batches(y_out[q])).then_inc(y_free[q], 16)

            def move_blocks(s):
                for k in range(KC):
                    sp.wait_ge(blocks_ready, 2 * s + k + 1)
                    sp.dma_start(bounce[:, :, k * RB * BK:(k + 1) * RB * BK],
                                 blocks[:, :, k].rearrange("p w b f -> p w (b f)")).then_inc(bounced, 16)
                sp.wait_ge(bounced, 16 * KC * (s + 1))
                for w in range(BP):
                    sp.dma_start(moved[w * BK:(w + 1) * BK].rearrange("i q k b f -> i q (k b f)"),
                                 bounce.rearrange("(q i) w e -> w i q e", i=BK)[w]).then_inc(moved_in, 16)

            def segment(pair, j, more=True):
                s, q = seg(pair, j), j % 2
                if j in (1, 2) and more:
                    load_next(pair, 1 - q)
                move_blocks(s - 1)
                if j == SEGS - 1:
                    store(pair, 0)
                if j == 0:
                    store(pair - 1, 1)

            with sp.Fori(0, PAIRS - 1) as pair:
                for j in range(1, SEGS):
                    segment(pair, j)
                segment(pair + 1, 0)
            for j in range(1, SEGS):
                segment(PAIRS - 1, j, more=False)
            for b in range(GB):
                sp.wait_ge(y_ready, GROUPS + b)
                sp.dma_start(out_rows[GROUPS - 1][:, b], batches(y_out[1])[:, b]).then_inc(y_free[1], 16)
            sp.wait_ge(y_free[0], 16 * (PAIRS + 1))
            sp.wait_ge(y_free[1], 16 * (PAIRS + GB))

        @block.gpsimd
        def _(pool):
            nc.gpsimd.memset(ident[:], 0.0).then_inc(ident_zero, 1)
            pool.wait_ge(ident_zero, 1)
            nc.gpsimd.affine_select(out=ident[:], in_=ident[:], compare_op=ALU.not_equal, fill=1.0, base=0,
                                    pattern=[[-1, P]], channel_multiplier=1).then_inc(ident_ready, 1)
            nc.gpsimd.memset(neg_half[:], -0.5).then_inc(ident_ready, 1)
            pool.wait_ge(ident_ready, 2)
            with pool.Fori(0, PAIRS) as pair:
                for q in range(2):
                    pool.wait_ge(stat_step, (2 * pair + q + 1) * STAT_STEPS)
                    nc.gpsimd.tensor_tensor(rstd[q][:], var[:], neg_half[:], ALU.pow).then_inc(rstd_ready, 1)

        @block.tensor
        def _(pe):
            def turn_matrix(i, rows):
                for k in range(KC):
                    for o in range(KC):
                        t = pe.transpose(mat_bank(i)[:, k, o * P:(o + 1) * P], rows(o, k), ident[:])
                t.then_inc(mat_turned, 1)

            def turn_new(group, q):
                pe.wait_ge(normed_ready, group + 1)
                for k in range(KC):
                    for b in range(RB):
                        t = pe.transpose(ps_t[:, k, b * P:(b + 1) * P], normed[q][:, b, k * P:(k + 1) * P], ident[:])
                    t.then_inc(turned, 1)

            def turn_last():
                pe.wait_ge(turn_taken, 2 * GROUPS)
                pe.wait_ge(hT_new, 2 * LAST + 2)
                for b in range(RB):
                    for k in range(KC):
                        at = (b % 2) * D + k * P
                        t = pe.transpose(ps_t[:, b // 2, at:at + P], hT[1][:, k, b * P:(b + 1) * P], ident[:])
                    if b % 2 == 1:
                        t.then_inc(turned, 1)

            def aggregate(pair, j, start):
                s, q = seg(pair, j), j % 2
                if start:
                    pe.wait_ge(mat_ready, ADJ + 1)
                    pe.wait_ge(bias_copied, 1)
                else:
                    pe.wait_ge(a_split, 2 * s)
                if j < 2:
                    pe.wait_ge(new_nat_split, 2 * pair + q + 1)
                for c in range(KC):
                    if j >= 2:
                        pe.wait_ge(nat_split, 2 * moved_before(pair, j) + c + 1)
                    cols = slice(c * P, (c + 1) * P)
                    for b in range(GB):
                        for m in range(NCH):
                            mm = triple(pe, ps_a[:, c, b * N:(b + 1) * N],
                                        nat_hi[q][:, b * NCH + m, cols], nat_lo[q][:, b * NCH + m, cols],
                                        mat_hi[:, ADJ, m, :], mat_lo[:, ADJ, m, :], m == 0, m == NCH - 1)
                    mm.then_inc(agg_done, 1)

            def segment(pair, j, tail=True, new=False):
                s, q = seg(pair, j), j % 2
                start = not tail
                if start:
                    aggregate(pair, j, start)
                    pe.wait_ge(w_summed, 2)
                    turn_matrix(W5, lambda o, k: w_sum["w5"][:, o, k * P:(k + 1) * P])
                    pe.wait_ge(mat_ready, U3 + 1)
                pe.wait_ge(hT_split, 2 * s + 2)
                for o in range(KC):
                    if tail:
                        pe.wait_ge(z_ready, 2 * (s - 1) + o + 1)
                    for k in range(KC):
                        if tail and (o, k) == (1,1):
                            aggregate(pair, j, start)
                        product(pe, ps_r, U3, o, hT_hi[q], hT_lo[q], k, k == 0, False)
                if start:
                    pe.wait_ge(mat_ready, W4 + 1)
                for k in range(KC):
                    pe.wait_ge(a_split, 2 * s + k + 1)
                    for o in range(KC):
                        mm = product(pe, ps_r, W4, o, a_hi, a_lo, k, False, k == KC - 1)
                        if k == KC - 1:
                            mm.then_inc(r_pre_done, 1)
                if tail:
                    pe.wait_ge(hv_ready, 2 * s)
                else:
                    pe.wait_ge(turn_taken, 2)
                    pe.wait_ge(w_summed, 4)
                    turn_matrix(W34, lambda o, k: w_diff[:, o, k * P:(k + 1) * P])
                    pe.wait_ge(loaded["u5"], 16)
                    turn_matrix(U5, lambda o, k: u_nat["u5"][:, o, k * P:(k + 1) * P])
                    pe.wait_ge(mat_ready, W5 + 1)
                for o in range(KC):
                    for k in range(KC):
                        product(pe, ps_h, W5, o, a_hi, a_lo, k, k == 0, False)
                if start:
                    pe.wait_ge(mat_ready, W34 + 1)
                for o in range(KC):
                    pe.wait_ge(r_ready, 2 * s + o + 1)
                    for k in range(KC):
                        mm = product(pe, ps_r, W34, o, a_hi, a_lo, k, False, k == KC - 1)
                    mm.then_inc(z_pre_done, 1)
                if start:
                    pe.wait_ge(mat_ready, U5 + 1)
                if new:
                    group = new_group(pair, j)
                    pe.wait_ge(turn_taken, 2 * group)
                    turn_new(group, 1 - q)
                for o in range(KC):
                    for k in range(KC):
                        if o == 0:
                            pe.wait_ge(rh_split, 2 * s + k + 1)
                        mm = product(pe, ps_h, U5, o, rh_hi, rh_lo, k, False, k == KC - 1)
                    mm.then_inc(hv_pre_done, 1)

            pe.wait_ge(ident_ready, 1)
            pe.wait_ge(b_loaded, 5 * 16)
            pe.transpose(ps_a[:, 0, 0:5 * KC], bias_rows[:], ident[0:5 * KC, 0:5 * KC]).then_inc(bias_turned, 1)
            pe.wait_ge(loaded["adj"], 16)
            turn_matrix(ADJ, lambda o, k: adj_nat[:, o, k:N:NCH])
            pe.wait_ge(loaded["u3"], 16)
            turn_matrix(U3, lambda o, k: u_nat["u3"][:, o, k * P:(k + 1) * P])
            turn_new(0, 0)
            pe.wait_ge(w_summed, 1)
            turn_matrix(W4, lambda o, k: w_sum["w4"][:, o, k * P:(k + 1) * P])

            segment(0, 0, tail=False, new=True)
            with pe.Fori(0, PAIRS - 1) as pair:
                for j in range(1, SEGS):
                    segment(pair, j, new=j == SEGS - 1)
                segment(pair + 1, 0, new=True)
            for j in range(1, SEGS):
                segment(PAIRS - 1, j)
            turn_last()

        @block.scalar
        def _(act):
            def split_new(group, q):
                act.wait_ge(normed_ready, group + 1)
                nc.scalar.activation(nat_hi[q][:], normed[q][:], ACT.Relu).then_inc(new_nat_hi_ready, 1)

            def take_new(q, group):
                for k in range(KC):
                    act.wait_ge(turned, 2 * group + k + 1)
                    nc.scalar.activation(hT_hi[q][:, k, :], ps_t[:, k, :], ACT.Relu).then_inc(hT_hi_ready, 1)
                    nc.scalar.activation(hT[q][:, k, :], ps_t[:, k, :], ACT.Relu).then_inc(turn_taken, 1)

            def split_matrix(i):
                act.wait_ge(mat_turned, i + 1)
                nc.scalar.activation(mat_hi[:, i], mat_bank(i), ACT.Copy).then_inc(mat_hi_ready, 1)

            def keep_x(pair, q, s):
                act.wait_ge(a_split, 2 * s)
                act.wait_ge(normed_ready, 2 * pair + q + 1)
                act.wait_ge(x_loaded[q], 16 * (pair + 1))
                nc.scalar.activation(x_keep[q][:], x_in[q][:], ACT.Copy).then_inc(x_kept[q], 1)

            def centre(pair, q):
                act.wait_ge(x_loaded[q], 16 * (pair + 1))
                act.wait_ge(rstd_ready, 2 * pair + q + 1)
                for b in range(RB):
                    last = nc.scalar.activation(normed[q][:, b, :], x_in[q][:, b, :], ACT.Identity,
                                                bias=neg_mean[q][:, b:b + 1])
                last.then_inc(centred, 1)

            def scale(pair, q):
                act.wait_ge(centred, 2 * (pair - 1) + q + 1)
                for b in range(RB):
                    last = nc.scalar.activation(normed[q][:, b, :], normed[q][:, b, :], ACT.Copy,
                                                scale=rstd[q][:, b:b + 1])
                last.then_inc(normed_ready, 1)

            def segment(pair, j, tail=True, new=False, more=True):
                s, q = seg(pair, j), j % 2
                last_step = j in (0, SEGS - 1)
                if j in (1, 2):
                    keep_x(pair, 1 - q, s)
                for c in range(KC):
                    act.wait_ge(agg_done, 2 * s + c + 1)
                    nc.scalar.activation(a_hi[:, c, :], ps_a[:, c, :], ACT.Copy).then_inc(a_hi_ready, 1)
                if not tail:
                    split_matrix(W5)
                if tail and not last_step:
                    act.wait_ge(hT_new, 2 * s)
                    nc.scalar.activation(hT_hi[1 - q][:], hT[1 - q][:], ACT.Copy).then_inc(hT_hi_ready, 2)
                if tail and new:
                    split_new(new_group(pair, j), 1 - q)
                if j in (3, 4) and more:
                    centre(pair + 1, 1 - q)
                if tail:
                    act.wait_ge(rh_ready, 2 * s)
                for o in range(KC):
                    act.wait_ge(r_pre_done, 2 * s + o + 1)
                    nc.scalar.activation(r[:, o, :], ps_r[:, o, :], ACT.Sigmoid,
                                         bias=bias_r[:, o:o + 1]).then_inc(r_ready, 1)
                if not tail:
                    split_matrix(W34)
                    split_matrix(U5)
                for c in range(KC):
                    act.wait_ge(rh_ready, 2 * s + c + 1)
                    nc.scalar.activation(rh_hi[:, c, :], rh[:, c, :], ACT.Copy).then_inc(rh_hi_ready, 1)
                if j in (3, 4) and more:
                    scale(pair + 1, 1 - q)
                if tail and not last_step:
                    act.wait_ge(moved_in, 16 * BP * s)
                    for k in range(KC):
                        nc.scalar.activation(chunk(nat_hi[1 - q], k), moved_chunk(k),
                                             ACT.Copy).then_inc(nat_hi_ready, 1)
                if not tail:
                    split_new(1, 1)
                if tail:
                    act.wait_ge(zdelta_ready, 2 * s)
                for o in range(KC):
                    act.wait_ge(z_pre_done, 2 * s + o + 1)
                    nc.scalar.activation(z[:, o, :], ps_r[:, o, :], ACT.Sigmoid,
                                         bias=bias_z[:, o:o + 1]).then_inc(z_ready, 1)
                if new:
                    if tail:
                        act.wait_ge(blocks_ready, 2 * s)
                    take_new(1 - q, new_group(pair, j))
                for o in range(KC):
                    act.wait_ge(hv_pre_done, 2 * s + o + 1)
                    nc.scalar.activation(hv[:, o, :], ps_h[:, o, :], ACT.Tanh,
                                         bias=bias_h[:, o:o + 1]).then_inc(hv_ready, 1)

            for i, b in enumerate((w3_b, u3_b, w4_b, w5_b, u5_b)):
                act.dma_start(bias_rows[i * KC:(i + 1) * KC, :], b.rearrange("(c p) -> c p", p=P)).then_inc(b_loaded, 16)
            act.wait_ge(ident_ready, 2)
            nc.scalar.activation(warm[:], neg_half[:, 0:1], ACT.Sigmoid).then_inc(tables_in, 1)
            split_matrix(ADJ)
            split_matrix(U3)
            split_new(0, 0)
            take_new(0, 0)
            split_matrix(W4)
            act.wait_ge(bias_ready, 3)
            segment(0, 0, tail=False, new=True)
            with act.Fori(0, PAIRS - 1) as pair:
                for j in range(1, SEGS):
                    segment(pair, j, new=j == SEGS - 1)
                segment(pair + 1, 0, new=True)
            for j in range(1, SEGS):
                segment(PAIRS - 1, j, more=False)

        @block.vector
        def _(dve):
            def measure(group, pair, q):
                step = lambda n: group * STAT_STEPS + n
                dve.wait_ge(x_loaded[q], 16 * (pair + 1))
                for b in range(RB):
                    last = nc.vector.bn_stats(stats[:, b, :], x_in[q][:, b, :])
                last.then_inc(stat_step, 1)
                dve.wait_ge(stat_step, step(1))
                nc.vector.tensor_tensor(mean2[:], stats[:, :, 1], stats[:, :, 4], ALU.add)
                nc.vector.tensor_tensor(mdiff[:], stats[:, :, 1], stats[:, :, 4], ALU.subtract)
                nc.vector.tensor_tensor(m2sum[:], stats[:, :, 2], stats[:, :, 5], ALU.add).then_inc(stat_step, 1)
                dve.wait_ge(stat_step, step(2))
                nc.vector.tensor_tensor(msq[:], mdiff[:], mdiff[:], ALU.mult).then_inc(stat_step, 1)
                nc.vector.tensor_scalar(neg_mean[q][:], mean2[:], -0.5, None, ALU.mult).then_inc(stat_step, 1)
                dve.wait_ge(stat_step, step(4))
                nc.vector.tensor_scalar(msq[:], msq[:], 0.25, EPS, ALU.mult, ALU.add).then_inc(stat_step, 1)
                dve.wait_ge(stat_step, step(5))
                nc.vector.scalar_tensor_tensor(out=var[:], in0=m2sum[:], scalar=1.0 / D, in1=msq[:],
                                               op0=ALU.mult, op1=ALU.add).then_inc(stat_step, 1)

            def normalise(group, q):
                dve.wait_ge(rstd_ready, group + 1)
                for b in range(RB):
                    last = nc.vector.tensor_scalar(normed[q][:, b, :], x_in[q][:, b, :], neg_mean[q][:, b:b + 1],
                                                   rstd[q][:, b:b + 1], ALU.add, ALU.mult)
                last.then_inc(normed_ready, 1)

            def split_new(group, q):
                dve.wait_ge(normed_ready, group + 1)
                dve.wait_ge(new_nat_hi_ready, group + 1)
                nc.vector.scalar_tensor_tensor(out=nat_lo[q][:], in0=normed[q][:], scalar=0.0, in1=bits(nat_hi[q][:]),
                                               op0=ALU.max, op1=ALU.subtract).then_inc(new_nat_split, 1)

            def split_matrix(i):
                dve.wait_ge(mat_hi_ready, i + 1)
                nc.vector.tensor_tensor(mat_lo[:, i], mat_bank(i), bits(mat_hi[:, i]),
                                        ALU.subtract).then_inc(mat_ready, 1)

            def take_new(q, s, group):
                for k in range(KC):
                    dve.wait_ge(hT_hi_ready, 2 * s + k + 1)
                    dve.wait_ge(turn_taken, 2 * group + k + 1)
                    nc.vector.tensor_tensor(hT_lo[q][:, k, :], hT[q][:, k, :], bits(hT_hi[q][:, k, :]),
                                            ALU.subtract).then_inc(hT_split, 1)

            def make_delta(s, q, c):
                dve.wait_ge(hv_ready, 2 * s + c + 1)
                nc.vector.tensor_tensor(delta[:, c, :], hv[:, c, :], hT[q][:, c, :],
                                        ALU.subtract).then_inc(delta_ready, 1)

            def make_zdelta(s, c):
                dve.wait_ge(delta_ready, 2 * s + c + 1)
                nc.vector.tensor_tensor(delta[:, c, :], z[:, c, :], delta[:, c, :],
                                        ALU.mult).then_inc(zdelta_ready, 1)

            def make_state(s, q, c):
                dve.wait_ge(zdelta_ready, 2 * s + c + 1)
                nc.vector.tensor_tensor(hT[q][:, c, :], hT[q][:, c, :], delta[:, c, :],
                                        ALU.add).then_inc(hT_new, 1)

            def split_a(s, c):
                dve.wait_ge(a_hi_ready, 2 * s + c + 1)
                nc.vector.tensor_tensor(a_lo[:, c, :], ps_a[:, c, :], bits(a_hi[:, c, :]),
                                        ALU.subtract).then_inc(a_split, 1)

            def split_state(s, q):
                dve.wait_ge(hT_hi_ready, 2 * s + 2)
                nc.vector.tensor_tensor(hT_lo[q][:], hT[q][:], bits(hT_hi[q][:]), ALU.subtract).then_inc(hT_split, 2)

            def make_blocks(s, q, k):
                dve.wait_ge(hT_new, 2 * s + k + 1)
                nc.vector.transpose(blocks[:, :, k].rearrange("p w b f -> p b w f"),
                                    hT[q][:, k, :].rearrange("p (b w i) -> p b w i", b=RB,
                                                             i=BK)).then_inc(blocks_ready, 1)

            def take_state(s, q, n):
                dve.wait_ge(moved_in, 16 * BP * (s + 1))
                for k in range(KC):
                    dve.wait_ge(nat_hi_ready, 2 * n + k + 1)
                    nc.vector.tensor_tensor(chunk(nat_lo[q], k), moved_chunk(k), chunk(bits(nat_hi[q][:]), k),
                                            ALU.subtract).then_inc(nat_split, 1)

            def add_x(pair, q, s):
                dve.wait_ge(y_free[q], 16 * (pair + 1))
                dve.wait_ge(moved_in, 16 * BP * (s + 1))
                for k in range(KC):
                    last = nc.vector.tensor_tensor(chunk(y_out[q], k), moved_chunk(k), chunk(x_keep[q], k), ALU.add)
                last.then_inc(y_ready, 1)

            def add_x_last():
                dve.wait_ge(y_free[1], 16 * PAIRS)
                for b in range(GB):
                    dve.wait_ge(turned, 2 * GROUPS + b + 1)
                    nc.vector.tensor_tensor(y_out[1][:, NCH * b:NCH * (b + 1), :],
                                            ps_t[:, b, :].rearrange("p (c d) -> p c d", d=D),
                                            x_keep[1][:, NCH * b:NCH * (b + 1), :], ALU.add).then_inc(y_ready, 1)

            def segment(pair, j, tail=True, new=False, more=True):
                s, q = seg(pair, j), j % 2
                last_step = j in (0, SEGS - 1)
                if tail:
                    make_delta(s - 1, 1 - q, 0)
                    make_zdelta(s - 1, 0)
                    make_delta(s - 1, 1 - q, 1)
                    make_state(s - 1, 1 - q, 0)
                    make_zdelta(s - 1, 1)
                    make_blocks(s - 1, 1 - q, 0)
                    make_state(s - 1, 1 - q, 1)
                    split_a(s, 0)
                    make_blocks(s - 1, 1 - q, 1)
                    split_a(s, 1)
                else:
                    for c in range(KC):
                        split_a(s, c)
                    split_matrix(W5)
                    measure(1, 0, 1)
                    normalise(1, 1)
                if tail and not last_step:
                    split_state(s + 1, 1 - q)
                if tail and new:
                    split_new(new_group(pair, j), 1 - q)
                for c in range(KC):
                    dve.wait_ge(r_ready, 2 * s + c + 1)
                    nc.vector.tensor_tensor(rh[:, c, :], r[:, c, :], hT[q][:, c, :], ALU.mult).then_inc(rh_ready, 1)
                if not tail:
                    split_matrix(W34)
                    split_matrix(U5)
                for c in range(KC):
                    dve.wait_ge(rh_hi_ready, 2 * s + c + 1)
                    nc.vector.tensor_tensor(rh_lo[:, c, :], rh[:, c, :], bits(rh_hi[:, c, :]),
                                            ALU.subtract).then_inc(rh_split, 1)
                if not tail:
                    split_new(1, 1)
                if j in (2, 3) and more:
                    measure(2 * (pair + 1) + q, pair + 1, q)
                if tail and not last_step:
                    take_state(s - 1, 1 - q, moved_before(pair, j + 1))
                elif tail:
                    add_x(pair if j else pair - 1, 1 - q, s - 1)
                if new:
                    take_new(1 - q, s + 1, new_group(pair, j))

            def sum_halves(k):
                dve.wait_ge(loaded[k], 16)
                nc.vector.tensor_tensor(w_sum[k][:], w_nat[k][:, :, 0:D], w_nat[k][:, :, D:2 * D],
                                        ALU.add).then_inc(w_summed, 1)

            measure(0, 0, 0)
            dve.wait_ge(bias_turned, 1)
            nc.vector.tensor_copy(bias_cols[:], ps_a[:, 0, 0:5 * KC]).then_inc(bias_copied, 1)
            dve.wait_ge(bias_copied, 1)
            b_w3, b_u3, b_w4, b_w5, b_u5 = (bias_cols[:, i * KC:(i + 1) * KC] for i in range(5))
            nc.vector.tensor_tensor(bias_z[:], b_w3, b_u3, ALU.add).then_inc(bias_ready, 1)
            nc.vector.tensor_tensor(bias_r[:], b_w4, b_u3, ALU.add).then_inc(bias_ready, 1)
            nc.vector.tensor_tensor(bias_h[:], b_w5, b_u5, ALU.add).then_inc(bias_ready, 1)
            normalise(0, 0)
            split_matrix(ADJ)
            split_matrix(U3)
            sum_halves("w4")
            split_new(0, 0)
            sum_halves("w5")
            take_new(0, 0, 0)
            sum_halves("w3")
            split_matrix(W4)
            dve.wait_ge(w_summed, 3)
            nc.vector.tensor_tensor(w_diff[:], w_sum["w3"][:], w_sum["w4"][:], ALU.subtract).then_inc(w_summed, 1)

            segment(0, 0, tail=False, new=True)
            with dve.Fori(0, PAIRS - 1) as pair:
                for j in range(1, SEGS):
                    segment(pair, j, new=j == SEGS - 1)
                segment(pair + 1, 0, new=True)
            for j in range(1, SEGS):
                segment(PAIRS - 1, j, more=False)
            for c in range(KC):
                make_delta(LAST, 1, c)
                make_zdelta(LAST, c)
                make_state(LAST, 1, c)
            add_x_last()


_INS = ["x", "adj", "L0_gnn_w3_w", "L0_gnn_w3_b", "L0_gnn_u3_w", "L0_gnn_u3_b", "L0_gnn_w4_w", "L0_gnn_w4_b",
        "L0_gnn_w5_w", "L0_gnn_w5_b", "L0_gnn_u5_w", "L0_gnn_u5_b"]


def kernel(**inputs):
    import numpy as _np
    import concourse.bacc as _bacc
    from concourse import mybir as _mybir
    from concourse.bass_utils import run_bass_kernel_spmd as _run

    nc = _bacc.Bacc("TRN2", target_bir_lowering=False, num_devices=1)
    arrays, args = {}, []
    for name in _INS:
        a = _np.ascontiguousarray(inputs[name])
        arrays[f"in_{name}"] = a
        args.append(nc.dram_tensor(f"in_{name}", a.shape, _mybir.dt.from_np(a.dtype), kind="ExternalInput").ap())
    x = inputs["x"]
    args.append(nc.dram_tensor("out_x", x.shape, _mybir.dt.from_np(_np.dtype("float32")), kind="ExternalOutput").ap())
    gnn_kernel(nc, *args)
    r = _run(nc, [arrays], core_ids=[0])
    return r.results[0]["out_x"]
```

```python
from contextlib import ExitStack

import concourse.bass as bass
from concourse import mybir

F32 = mybir.dt.float32
F32R = mybir.dt.float32r
ALU = mybir.AluOpType
ACT = mybir.ActivationFunctionType

P = 128
EPS = 1e-5

ADJ, U3, W4, W5, W34, U5 = range(6)


def gnn_kernel(nc, x, adj, w3_w, w3_b, u3_w, u3_b, w4_w, w4_b, w5_w, w5_b, u5_w, u5_b, out):
    NBATCH, N, D = x.shape
    STEPS = 3
    GB = 512 // N
    ROWS = GB * N
    KC = D // P
    NCH = N // P
    RB = GB * NCH
    GROUPS = NBATCH // GB
    PAIRS = GROUPS // 2
    SEGS = 2 * STEPS
    LAST = PAIRS * SEGS - 1
    BK = 32
    BP = P // BK
    assert D == 256 and N == 256 and GROUPS % 2 == 0

    x_rows = x.rearrange("(g b) (p c) d -> g p b (c d)", b=GB, c=NCH)
    out_rows = out.rearrange("(g b) (p c) d -> g p b (c d)", b=GB, c=NCH)

    with ExitStack() as ctx:
        def sb(name, shape, dt=F32):
            return ctx.enter_context(nc.sbuf_tensor(name, shape, dt))

        def psum(name, shape):
            return ctx.enter_context(nc.psum_tensor(name, shape, F32))

        def sem(name):
            return ctx.enter_context(nc.semaphore(name))

        ident = sb("ident", [P, P])
        neg_half = sb("neg_half", [P, RB])
        warm = sb("warm", [P, 1])
        w_nat = {k: sb(f"{k}_nat", [P, KC, 2 * D]) for k in ("w3", "w4", "w5")}
        u_nat = {k: sb(f"{k}_nat", [P, KC, D]) for k in ("u3", "u5")}
        adj_nat = sb("adj_nat", [P, NCH, N])
        w_sum = {k: sb(f"{k}_sum", [P, KC, D]) for k in ("w3", "w4", "w5")}
        w_diff = sb("w_diff", [P, KC, D])
        mat_hi = sb("mat_hi", [P, 6, KC, D], F32R)
        mat_lo = sb("mat_lo", [P, 6, KC, D], F32R)
        bias_rows = sb("bias_rows", [5 * KC, P])
        bias_cols = sb("bias_cols", [P, 5 * KC])
        bias_z = sb("bias_z", [P, KC])
        bias_r = sb("bias_r", [P, KC])
        bias_h = sb("bias_h", [P, KC])
        x_in = [sb(f"x_in{q}", [P, RB, D]) for q in range(2)]
        x_keep = [sb(f"x_keep{q}", [P, RB, D]) for q in range(2)]
        normed = [sb(f"normed{q}", [P, RB, D]) for q in range(2)]
        nat_hi = [sb(f"nat_hi{q}", [P, RB, D], F32R) for q in range(2)]
        nat_lo = [sb(f"nat_lo{q}", [P, RB, D], F32R) for q in range(2)]
        hT = [sb(f"hT{q}", [P, KC, ROWS]) for q in range(2)]
        hT_hi = [sb(f"hT_hi{q}", [P, KC, ROWS], F32R) for q in range(2)]
        hT_lo = [sb(f"hT_lo{q}", [P, KC, ROWS], F32R) for q in range(2)]
        y_out = [sb(f"y_out{q}", [P, RB, D]) for q in range(2)]
        a_hi = sb("a_hi", [P, KC, ROWS], F32R)
        a_lo = sb("a_lo", [P, KC, ROWS], F32R)
        r = sb("r", [P, KC, ROWS])
        rh = sb("rh", [P, KC, ROWS])
        rh_hi = sb("rh_hi", [P, KC, ROWS], F32R)
        rh_lo = sb("rh_lo", [P, KC, ROWS], F32R)
        z = sb("z", [P, KC, ROWS])
        hv = sb("hv", [P, KC, ROWS])
        delta = sb("delta", [P, KC, ROWS])
        blocks = sb("blocks", [P, BP, KC, RB, BK])
        moved = sb("moved", [P, BP, KC, RB, BK])
        bounce = nc.dram_tensor("bounce", [P, BP, KC * RB * BK], F32, kind="Internal").ap()
        new_blocks = sb("new_blocks", [P, BP, KC, RB, BK])
        new_moved = sb("new_moved", [P, BP, KC, RB, BK])
        new_bounce = nc.dram_tensor("new_bounce", [P, BP, KC * RB * BK], F32, kind="Internal").ap()
        stats = sb("stats", [P, RB, 6])
        mean2 = sb("mean2", [P, RB])
        mdiff = sb("mdiff", [P, RB])
        msq = sb("msq", [P, RB])
        m2sum = sb("m2sum", [P, RB])
        var = sb("var", [P, RB])
        neg_mean = [sb(f"neg_mean{q}", [P, RB]) for q in range(2)]
        rstd = [sb(f"rstd{q}", [P, RB]) for q in range(2)]

        ps_a = psum("ps_a", [P, KC, ROWS])
        ps_r = psum("ps_r", [P, KC, ROWS])
        ps_h = psum("ps_h", [P, KC, ROWS])
        ps_t = psum("ps_t", [P, 2, ROWS])

        loaded = {k: sem(f"{k}_loaded") for k in ("adj", "u3", "w4", "w5", "w3", "u5")}
        b_loaded = sem("b_loaded")
        x0_first = sem("x0_first")
        x_loaded = [sem("x_loaded_a"), sem("x_loaded_b")]
        y_free = [sem("y_free_a"), sem("y_free_b")]
        ident_zero = sem("ident_zero")
        ident_ready = sem("ident_ready")
        w_summed = sem("w_summed")
        mat_turned = sem("mat_turned")
        mat_hi_ready = sem("mat_hi_ready")
        mat_ready = sem("mat_ready")
        bias_turned = sem("bias_turned")
        bias_copied = sem("bias_copied")
        bias_ready = sem("bias_ready")
        tables_in = sem("tables_in")
        agg_done = sem("agg_done")
        r_pre_done = sem("r_pre_done")
        z_pre_done = sem("z_pre_done")
        hv_pre_done = sem("hv_pre_done")
        a_hi_ready = sem("a_hi_ready")
        a_split = sem("a_split")
        r_ready = sem("r_ready")
        z_ready = sem("z_ready")
        hv_ready = sem("hv_ready")
        rh_ready = sem("rh_ready")
        rh_hi_ready = sem("rh_hi_ready")
        rh_split = sem("rh_split")
        delta_ready = sem("delta_ready")
        zdelta_ready = sem("zdelta_ready")
        hT_new = sem("hT_new")
        hT_hi_ready = sem("hT_hi_ready")
        hT_split = sem("hT_split")
        blocks_ready = sem("blocks_ready")
        nat_hi_ready = sem("nat_hi_ready")
        nat_split = sem("nat_split")
        bounced = sem("bounced")
        moved_in = sem("moved_in")
        new_blocks_ready = sem("new_blocks_ready")
        new_bounced = sem("new_bounced")
        new_moved_in = sem("new_moved_in")
        new_hT_ready = sem("new_hT_ready")
        turned = sem("turned")
        stat_step = sem("stat_step")
        rstd_ready = sem("rstd_ready")
        centred = sem("centred")
        normed_ready = sem("normed_ready")
        new_nat_hi_ready = sem("new_nat_hi_ready")
        new_nat_split = sem("new_nat_split")
        y_ready = sem("y_ready")
        x_kept = [sem("x_kept_a"), sem("x_kept_b")]

        def seg(pair, j):
            return pair * SEGS + j

        def feature_chunk(t, k):
            return t[:, k, :].rearrange("p (b w i) -> p b w i", b=RB, i=BK)

        def moved_before(pair, j):
            return pair * (SEGS - 2) + j - 2

        def new_group(pair, j):
            return 2 * pair + (1 if j == 0 else 2)

        STAT_STEPS = 6

        def triple(pe, dst, st_hi, st_lo, mv_hi, mv_lo, first, last):
            pe.matmul(dst, st_hi, mv_hi, start=first, stop=False, skip_group_check=True)
            pe.matmul(dst, st_hi, mv_lo, start=False, stop=False, skip_group_check=True)
            return pe.matmul(dst, st_lo, mv_hi, start=False, stop=last, skip_group_check=True)

        def product(pe, dst, mat, o, mv_hi, mv_lo, k, first, last):
            cols = slice(o * P, (o + 1) * P)
            return triple(pe, dst[:, o, :], mat_hi[:, mat, k, cols], mat_lo[:, mat, k, cols],
                          mv_hi[:, k, :], mv_lo[:, k, :], first, last)

        def mat_bank(i):
            return (ps_r, ps_h, ps_t)[i // 2][:, i % 2, :].rearrange("p (k o) -> p k o", k=KC)

        def turned_chunk(k):
            return ps_t[:, k, :].rearrange("p (b f) -> p b f", f=P)

        def moved_chunk(k):
            return moved[:, :, k].rearrange("p q b f -> p b q f")

        def chunk(t, k):
            return t[:, :, k * P:(k + 1) * P].rearrange("p b (q f) -> p b q f", f=BK)

        def bits(t):
            return t.bitcast(F32)

        block = ctx.enter_context(nc.Block())

        @block.sync
        def _(sp):
            def batches(t):
                return t[:].rearrange("p (b c) d -> p b (c d)", b=GB)

            for q in range(2):
                sp.sem_inc(y_free[q], 16)
            sp.dma_start(batches(x_in[0])[:, 0], x_rows[0][:, 0]).then_inc(x0_first, 16)
            sp.dma_start(batches(x_in[0])[:, 1:], x_rows[0][:, 1:]).then_inc(x_loaded[0], 16)
            sp.dma_start(adj_nat[:], adj.rearrange("(p c) m -> p c m", c=NCH)).then_inc(loaded["adj"], 16)
            for k, w, t in (("u3", u3_w, u_nat["u3"]), ("w4", w4_w, w_nat["w4"]), ("w5", w5_w, w_nat["w5"]),
                            ("w3", w3_w, w_nat["w3"]), ("u5", u5_w, u_nat["u5"])):
                sp.dma_start(t[:], w.rearrange("(c p) d -> p c d", p=P)).then_inc(loaded[k], 16)
            sp.dma_start(batches(x_in[1]), x_rows[1]).then_inc(x_loaded[1], 16)

            PARTS = sorted(range(BP), key=lambda w: w % (BP // 2))

            def load_next(pair, q):
                sp.wait_ge(x_kept[q], pair + 1)
                sp.dma_start(batches(x_in[q]), x_rows[2 * (pair + 1) + q]).then_inc(x_loaded[q], 16)

            def store(pair, q):
                sp.wait_ge(y_ready, 2 * pair + q + 1)
                sp.dma_start(out_rows[2 * pair + q], batches(y_out[q])).then_inc(y_free[q], 16)

            def move_blocks(s):
                for k in range(KC):
                    sp.wait_ge(blocks_ready, 2 * s + k + 1)
                    sp.dma_start(bounce[:, :, k * RB * BK:(k + 1) * RB * BK],
                                 blocks[:, :, k].rearrange("p w b f -> p w (b f)")).then_inc(bounced, 16)
                sp.wait_ge(bounced, 16 * KC * (s + 1))
                for w in PARTS:
                    sp.dma_start(moved[w * BK:(w + 1) * BK].rearrange("i q k b f -> i q (k b f)"),
                                 bounce.rearrange("(q i) w e -> w i q e", i=BK)[w]).then_inc(moved_in, 16)

            def bounce_new(group):
                sp.wait_ge(new_blocks_ready, group - 1)
                sp.dma_start(new_bounce, new_blocks[:].rearrange("p q k b i -> p q (k b i)")).then_inc(new_bounced, 16)

            def move_new(group):
                sp.wait_ge(new_bounced, 16 * (group - 1))
                for q in PARTS:
                    sp.dma_start(new_moved[q * BK:(q + 1) * BK].rearrange("f w k b i -> f w (k b i)"),
                                 new_bounce.rearrange("(w f) q e -> q f w e", f=BK)[q]).then_inc(new_moved_in, 16)

            def segment(pair, j, more=True):
                s, q = seg(pair, j), j % 2
                if j in (1, 2) and more:
                    load_next(pair, 1 - q)
                if j == 0 or j == SEGS - 1 and more:
                    move_new(new_group(pair, j))
                move_blocks(s - 1)
                if j >= SEGS - 2 and more:
                    bounce_new(2 * (pair + 1) + q)
                if j == SEGS - 1:
                    store(pair, 0)
                if j == 0:
                    store(pair - 1, 1)

            with sp.Fori(0, PAIRS - 1) as pair:
                for j in range(1, SEGS):
                    segment(pair, j)
                segment(pair + 1, 0)
            for j in range(1, SEGS):
                segment(PAIRS - 1, j, more=False)
            for b in range(GB):
                sp.wait_ge(y_ready, GROUPS + b)
                sp.dma_start(out_rows[GROUPS - 1][:, b], batches(y_out[1])[:, b]).then_inc(y_free[1], 16)
            sp.wait_ge(y_free[0], 16 * (PAIRS + 1))
            sp.wait_ge(y_free[1], 16 * (PAIRS + GB))

        @block.gpsimd
        def _(pool):
            nc.gpsimd.memset(ident[:], 0.0).then_inc(ident_zero, 1)
            pool.wait_ge(ident_zero, 1)
            nc.gpsimd.affine_select(out=ident[:], in_=ident[:], compare_op=ALU.not_equal, fill=1.0, base=0,
                                    pattern=[[-1, P]], channel_multiplier=1).then_inc(ident_ready, 1)
            nc.gpsimd.memset(neg_half[:], -0.5).then_inc(ident_ready, 1)
            pool.wait_ge(ident_ready, 2)
            with pool.Fori(0, PAIRS) as pair:
                for q in range(2):
                    pool.wait_ge(stat_step, (2 * pair + q + 1) * STAT_STEPS)
                    nc.gpsimd.tensor_tensor(rstd[q][:], var[:], neg_half[:], ALU.pow).then_inc(rstd_ready, 1)

        @block.tensor
        def _(pe):
            def turn_matrix(i, rows):
                for k in range(KC):
                    for o in range(KC):
                        t = pe.transpose(mat_bank(i)[:, k, o * P:(o + 1) * P], rows(o, k), ident[:])
                t.then_inc(mat_turned, 1)

            def turn_first(group):
                pe.wait_ge(normed_ready, group + 1)
                for k in range(KC):
                    for b in range(RB):
                        t = pe.transpose(ps_t[:, k, b * P:(b + 1) * P], normed[group][:, b, k * P:(k + 1) * P], ident[:])
                    t.then_inc(turned, 1)

            def turn_last():
                pe.wait_ge(new_hT_ready, 2 * 2)
                for k in range(KC):
                    pe.wait_ge(hT_new, 2 * LAST + k + 1)
                    for b in range(RB):
                        t = pe.transpose(ps_t[:, k, b * P:(b + 1) * P], hT[1][:, k, b * P:(b + 1) * P], ident[:])
                    t.then_inc(turned, 1)

            def aggregate(pair, j, start):
                s, q = seg(pair, j), j % 2
                if start:
                    pe.wait_ge(mat_ready, ADJ + 1)
                else:
                    pe.wait_ge(a_split, 2 * s)
                if j < 2:
                    pe.wait_ge(new_nat_split, 2 * pair + q + 1)
                for c in range(KC):
                    if j >= 2:
                        pe.wait_ge(nat_split, 2 * moved_before(pair, j) + c + 1)
                    cols = slice(c * P, (c + 1) * P)
                    for b in range(GB):
                        for m in range(NCH):
                            mm = triple(pe, ps_a[:, c, b * N:(b + 1) * N],
                                        nat_hi[q][:, b * NCH + m, cols], nat_lo[q][:, b * NCH + m, cols],
                                        mat_hi[:, ADJ, m, :], mat_lo[:, ADJ, m, :], m == 0, m == NCH - 1)
                    mm.then_inc(agg_done, 1)

            def segment(pair, j, tail=True):
                s, q = seg(pair, j), j % 2
                start = not tail
                if start:
                    aggregate(pair, j, start)
                    pe.wait_ge(w_summed, 2)
                    pe.wait_ge(bias_copied, 1)
                    turn_matrix(W5, lambda o, k: w_sum["w5"][:, o, k * P:(k + 1) * P])
                    pe.wait_ge(mat_ready, U3 + 1)
                pe.wait_ge(hT_split, 2 * s + 2)
                for o in range(KC):
                    if tail:
                        pe.wait_ge(z_ready, 2 * (s - 1) + o + 1)
                    for k in range(KC):
                        if tail and (o, k) == (KC - 1, KC - 1):
                            aggregate(pair, j, start)
                        product(pe, ps_r, U3, o, hT_hi[q], hT_lo[q], k, k == 0, False)
                if start:
                    pe.wait_ge(mat_ready, W4 + 1)
                for k in range(KC):
                    pe.wait_ge(a_split, 2 * s + k + 1)
                    for o in range(KC):
                        mm = product(pe, ps_r, W4, o, a_hi, a_lo, k, False, k == KC - 1)
                        if k == KC - 1:
                            mm.then_inc(r_pre_done, 1)
                if tail:
                    pe.wait_ge(hv_ready, 2 * s)
                else:
                    pe.wait_ge(new_hT_ready, 2)
                    pe.wait_ge(w_summed, 4)
                    turn_matrix(W34, lambda o, k: w_diff[:, o, k * P:(k + 1) * P])
                    pe.wait_ge(loaded["u5"], 16)
                    turn_matrix(U5, lambda o, k: u_nat["u5"][:, o, k * P:(k + 1) * P])
                    pe.wait_ge(mat_ready, W5 + 1)
                for o in range(KC):
                    for k in range(KC):
                        product(pe, ps_h, W5, o, a_hi, a_lo, k, k == 0, False)
                if start:
                    pe.wait_ge(mat_ready, W34 + 1)
                for o in range(KC):
                    pe.wait_ge(r_ready, 2 * s + o + 1)
                    for k in range(KC):
                        mm = product(pe, ps_r, W34, o, a_hi, a_lo, k, False, k == KC - 1)
                    mm.then_inc(z_pre_done, 1)
                if start:
                    pe.wait_ge(mat_ready, U5 + 1)
                    turn_first(1)
                for o in range(KC):
                    for k in range(KC):
                        if o == 0:
                            pe.wait_ge(rh_split, 2 * s + k + 1)
                        mm = product(pe, ps_h, U5, o, rh_hi, rh_lo, k, False, k == KC - 1)
                    mm.then_inc(hv_pre_done, 1)

            pe.wait_ge(ident_ready, 1)
            pe.wait_ge(loaded["adj"], 16)
            turn_matrix(ADJ, lambda o, k: adj_nat[:, o, k:N:NCH])
            pe.wait_ge(loaded["u3"], 16)
            turn_matrix(U3, lambda o, k: u_nat["u3"][:, o, k * P:(k + 1) * P])
            turn_first(0)
            pe.wait_ge(w_summed, 1)
            turn_matrix(W4, lambda o, k: w_sum["w4"][:, o, k * P:(k + 1) * P])
            pe.wait_ge(b_loaded, 5 * 16)
            pe.transpose(ps_h[:, 1, 0:5 * KC], bias_rows[:], ident[0:5 * KC, 0:5 * KC]).then_inc(bias_turned, 1)

            segment(0, 0, tail=False)
            with pe.Fori(0, PAIRS - 1) as pair:
                for j in range(1, SEGS):
                    segment(pair, j)
                segment(pair + 1, 0)
            for j in range(1, SEGS):
                segment(PAIRS - 1, j)
            turn_last()

        @block.scalar
        def _(act):
            def split_new(group, q):
                act.wait_ge(normed_ready, group + 1)
                nc.scalar.activation(nat_hi[q][:], normed[q][:], ACT.Relu).then_inc(new_nat_hi_ready, 1)

            def take_first(group):
                for k in range(KC):
                    act.wait_ge(turned, 2 * group + k + 1)
                    nc.scalar.activation(hT_hi[group][:, k, :], ps_t[:, k, :], ACT.Relu).then_inc(hT_hi_ready, 1)
                    nc.scalar.activation(hT[group][:, k, :], ps_t[:, k, :], ACT.Relu).then_inc(new_hT_ready, 1)

            def take_new(s, q, group):
                act.wait_ge(new_moved_in, 16 * BP * (group - 1))
                act.wait_ge(blocks_ready, 2 * s)
                for k in range(KC):
                    moved_k = new_moved[:, :, k].rearrange("p w b i -> p b w i")
                    nc.scalar.activation(feature_chunk(hT_hi[q], k), moved_k, ACT.Relu).then_inc(hT_hi_ready, 1)
                    nc.scalar.activation(feature_chunk(hT[q], k), moved_k, ACT.Relu).then_inc(new_hT_ready, 1)

            def split_matrix(i):
                act.wait_ge(mat_turned, i + 1)
                nc.scalar.activation(mat_hi[:, i], mat_bank(i), ACT.Copy).then_inc(mat_hi_ready, 1)

            def keep_x(pair, q, s):
                act.wait_ge(a_split, 2 * s)
                act.wait_ge(normed_ready, 2 * pair + q + 1)
                act.wait_ge(x_loaded[q], 16 * (pair + 1))
                nc.scalar.activation(x_keep[q][:], x_in[q][:], ACT.Copy).then_inc(x_kept[q], 1)

            def centre(pair, q):
                act.wait_ge(x_loaded[q], 16 * (pair + 1))
                act.wait_ge(rstd_ready, 2 * pair + q + 1)
                for b in range(RB):
                    last = nc.scalar.activation(normed[q][:, b, :], x_in[q][:, b, :], ACT.Identity,
                                                bias=neg_mean[q][:, b:b + 1])
                last.then_inc(centred, 1)

            def scale(pair, q):
                act.wait_ge(centred, 2 * (pair - 1) + q + 1)
                for b in range(RB):
                    last = nc.scalar.activation(normed[q][:, b, :], normed[q][:, b, :], ACT.Copy,
                                                scale=rstd[q][:, b:b + 1])
                last.then_inc(normed_ready, 1)

            def segment(pair, j, tail=True, new=False, more=True):
                s, q = seg(pair, j), j % 2
                last_step = j in (0, SEGS - 1)
                if j in (1, 2):
                    keep_x(pair, 1 - q, s)
                for c in range(KC):
                    act.wait_ge(agg_done, 2 * s + c + 1)
                    nc.scalar.activation(a_hi[:, c, :], ps_a[:, c, :], ACT.Copy).then_inc(a_hi_ready, 1)
                if not tail:
                    split_matrix(W5)
                if tail and not last_step:
                    act.wait_ge(hT_new, 2 * s)
                    nc.scalar.activation(hT_hi[1 - q][:], hT[1 - q][:], ACT.Copy).then_inc(hT_hi_ready, 2)
                if tail and new:
                    split_new(new_group(pair, j), 1 - q)
                if j in (3, 4) and more:
                    centre(pair + 1, 1 - q)
                if tail:
                    act.wait_ge(rh_ready, 2 * s)
                for o in range(KC):
                    act.wait_ge(r_pre_done, 2 * s + o + 1)
                    nc.scalar.activation(r[:, o, :], ps_r[:, o, :], ACT.Sigmoid,
                                         bias=bias_r[:, o:o + 1]).then_inc(r_ready, 1)
                if not tail:
                    split_matrix(W34)
                    split_matrix(U5)
                for c in range(KC):
                    act.wait_ge(rh_ready, 2 * s + c + 1)
                    nc.scalar.activation(rh_hi[:, c, :], rh[:, c, :], ACT.Copy).then_inc(rh_hi_ready, 1)
                if j in (3, 4) and more:
                    scale(pair + 1, 1 - q)
                if tail and not last_step:
                    act.wait_ge(moved_in, 16 * BP * s)
                    for k in range(KC):
                        nc.scalar.activation(chunk(nat_hi[1 - q], k), moved_chunk(k),
                                             ACT.Copy).then_inc(nat_hi_ready, 1)
                if tail and new:
                    take_new(s, 1 - q, new_group(pair, j))
                if not tail:
                    split_new(1, 1)
                if tail:
                    act.wait_ge(zdelta_ready, 2 * s)
                for o in range(KC):
                    act.wait_ge(z_pre_done, 2 * s + o + 1)
                    nc.scalar.activation(z[:, o, :], ps_r[:, o, :], ACT.Sigmoid,
                                         bias=bias_z[:, o:o + 1]).then_inc(z_ready, 1)
                if not tail:
                    take_first(1)
                for o in range(KC):
                    act.wait_ge(hv_pre_done, 2 * s + o + 1)
                    nc.scalar.activation(hv[:, o, :], ps_h[:, o, :], ACT.Tanh,
                                         bias=bias_h[:, o:o + 1]).then_inc(hv_ready, 1)

            act.wait_ge(ident_ready, 2)
            nc.scalar.activation(warm[:], neg_half[:, 0:1], ACT.Sigmoid).then_inc(tables_in, 1)
            for i, b in enumerate((w3_b, u3_b, w4_b, w5_b, u5_b)):
                act.dma_start(bias_rows[i * KC:(i + 1) * KC, :], b.rearrange("(c p) -> c p", p=P)).then_inc(b_loaded, 16)
            split_matrix(ADJ)
            split_matrix(U3)
            split_new(0, 0)
            take_first(0)
            split_matrix(W4)
            act.wait_ge(bias_ready, 3)
            segment(0, 0, tail=False, new=True)
            with act.Fori(0, PAIRS - 1) as pair:
                for j in range(1, SEGS):
                    segment(pair, j, new=j == SEGS - 1)
                segment(pair + 1, 0, new=True)
            for j in range(1, SEGS):
                segment(PAIRS - 1, j, more=False)

        @block.vector
        def _(dve):
            def measure(group, pair, q, first=False):
                step = lambda n: group * STAT_STEPS + n
                if first:
                    dve.wait_ge(x0_first, 16)
                else:
                    dve.wait_ge(x_loaded[q], 16 * (pair + 1))
                for b in range(RB):
                    if first and b == NCH:
                        dve.wait_ge(x_loaded[q], 16)
                    last = nc.vector.bn_stats(stats[:, b, :], x_in[q][:, b, :])
                last.then_inc(stat_step, 1)
                dve.wait_ge(stat_step, step(1))
                nc.vector.tensor_tensor(mean2[:], stats[:, :, 1], stats[:, :, 4], ALU.add)
                nc.vector.tensor_tensor(mdiff[:], stats[:, :, 1], stats[:, :, 4], ALU.subtract)
                nc.vector.tensor_tensor(m2sum[:], stats[:, :, 2], stats[:, :, 5], ALU.add).then_inc(stat_step, 1)
                dve.wait_ge(stat_step, step(2))
                nc.vector.tensor_tensor(msq[:], mdiff[:], mdiff[:], ALU.mult).then_inc(stat_step, 1)
                nc.vector.tensor_scalar(neg_mean[q][:], mean2[:], -0.5, None, ALU.mult).then_inc(stat_step, 1)
                dve.wait_ge(stat_step, step(4))
                nc.vector.tensor_scalar(msq[:], msq[:], 0.25, EPS, ALU.mult, ALU.add).then_inc(stat_step, 1)
                dve.wait_ge(stat_step, step(5))
                nc.vector.scalar_tensor_tensor(out=var[:], in0=m2sum[:], scalar=1.0 / D, in1=msq[:],
                                               op0=ALU.mult, op1=ALU.add).then_inc(stat_step, 1)

            def normalise(group, q):
                dve.wait_ge(rstd_ready, group + 1)
                for b in range(RB):
                    last = nc.vector.tensor_scalar(normed[q][:, b, :], x_in[q][:, b, :], neg_mean[q][:, b:b + 1],
                                                   rstd[q][:, b:b + 1], ALU.add, ALU.mult)
                last.then_inc(normed_ready, 1)

            def split_new(group, q):
                dve.wait_ge(normed_ready, group + 1)
                dve.wait_ge(new_nat_hi_ready, group + 1)
                nc.vector.scalar_tensor_tensor(out=nat_lo[q][:], in0=normed[q][:], scalar=0.0, in1=bits(nat_hi[q][:]),
                                               op0=ALU.max, op1=ALU.subtract).then_inc(new_nat_split, 1)

            def split_matrix(i):
                dve.wait_ge(mat_hi_ready, i + 1)
                nc.vector.tensor_tensor(mat_lo[:, i], mat_bank(i), bits(mat_hi[:, i]),
                                        ALU.subtract).then_inc(mat_ready, 1)

            def take_new(q, s, group):
                for k in range(KC):
                    dve.wait_ge(hT_hi_ready, 2 * s + k + 1)
                    dve.wait_ge(new_hT_ready, 2 * group + k + 1)
                    nc.vector.tensor_tensor(hT_lo[q][:, k, :], hT[q][:, k, :], bits(hT_hi[q][:, k, :]),
                                            ALU.subtract).then_inc(hT_split, 1)

            def make_delta(s, q, c):
                dve.wait_ge(hv_ready, 2 * s + c + 1)
                nc.vector.tensor_tensor(delta[:, c, :], hv[:, c, :], hT[q][:, c, :],
                                        ALU.subtract).then_inc(delta_ready, 1)

            def make_zdelta(s, c):
                dve.wait_ge(delta_ready, 2 * s + c + 1)
                nc.vector.tensor_tensor(delta[:, c, :], z[:, c, :], delta[:, c, :],
                                        ALU.mult).then_inc(zdelta_ready, 1)

            def make_state(s, q, c):
                dve.wait_ge(zdelta_ready, 2 * s + c + 1)
                nc.vector.tensor_tensor(hT[q][:, c, :], hT[q][:, c, :], delta[:, c, :],
                                        ALU.add).then_inc(hT_new, 1)

            def split_a(s, c):
                dve.wait_ge(a_hi_ready, 2 * s + c + 1)
                nc.vector.tensor_tensor(a_lo[:, c, :], ps_a[:, c, :], bits(a_hi[:, c, :]),
                                        ALU.subtract).then_inc(a_split, 1)

            def split_state(s, q):
                dve.wait_ge(hT_hi_ready, 2 * s + 2)
                nc.vector.tensor_tensor(hT_lo[q][:], hT[q][:], bits(hT_hi[q][:]), ALU.subtract).then_inc(hT_split, 2)

            def make_blocks(s, q, k):
                dve.wait_ge(hT_new, 2 * s + k + 1)
                nc.vector.transpose(blocks[:, :, k].rearrange("p w b f -> p b w f"),
                                    feature_chunk(hT[q], k)).then_inc(blocks_ready, 1)

            def make_new_blocks(group, q):
                dve.wait_ge(normed_ready, group + 1)
                dve.wait_ge(new_hT_ready, 2 * group)
                for k in range(KC):
                    last = nc.vector.transpose(new_blocks[:, :, k].rearrange("p q b i -> p b q i"),
                                               chunk(normed[q], k))
                last.then_inc(new_blocks_ready, 1)

            def take_state(s, q, n):
                dve.wait_ge(moved_in, 16 * BP * (s + 1))
                for k in range(KC):
                    dve.wait_ge(nat_hi_ready, 2 * n + k + 1)
                    nc.vector.tensor_tensor(chunk(nat_lo[q], k), moved_chunk(k), chunk(bits(nat_hi[q][:]), k),
                                            ALU.subtract).then_inc(nat_split, 1)

            def add_x(pair, q, s):
                dve.wait_ge(y_free[q], 16 * (pair + 1))
                dve.wait_ge(moved_in, 16 * BP * (s + 1))
                for k in range(KC):
                    last = nc.vector.tensor_tensor(chunk(y_out[q], k), moved_chunk(k), chunk(x_keep[q], k), ALU.add)
                last.then_inc(y_ready, 1)

            def add_x_last():
                dve.wait_ge(y_free[1], 16 * PAIRS)
                for k in range(KC):
                    dve.wait_ge(turned, 2 * 2 + k + 1)
                    cols = slice(k * P, (k + 1) * P)
                    at_once = RB if k < KC - 1 else NCH
                    for b in range(0, RB, at_once):
                        add = nc.vector.tensor_tensor(y_out[1][:, b:b + at_once, cols],
                                                      turned_chunk(k)[:, b:b + at_once],
                                                      x_keep[1][:, b:b + at_once, cols], ALU.add)
                        if k == KC - 1:
                            add.then_inc(y_ready, 1)

            def segment(pair, j, tail=True, new=False, more=True):
                s, q = seg(pair, j), j % 2
                last_step = j in (0, SEGS - 1)
                if tail:
                    make_delta(s - 1, 1 - q, 0)
                    make_zdelta(s - 1, 0)
                    make_delta(s - 1, 1 - q, 1)
                    make_state(s - 1, 1 - q, 0)
                    make_zdelta(s - 1, 1)
                    make_blocks(s - 1, 1 - q, 0)
                    make_state(s - 1, 1 - q, 1)
                    split_a(s, 0)
                    make_blocks(s - 1, 1 - q, 1)
                    split_a(s, 1)
                else:
                    for c in range(KC):
                        split_a(s, c)
                    split_matrix(W5)
                    measure(1, 0, 1)
                    normalise(1, 1)
                    split_matrix(W34)
                if tail and not last_step:
                    split_state(s + 1, 1 - q)
                if tail and new:
                    split_new(new_group(pair, j), 1 - q)
                for c in range(KC):
                    dve.wait_ge(r_ready, 2 * s + c + 1)
                    nc.vector.tensor_tensor(rh[:, c, :], r[:, c, :], hT[q][:, c, :], ALU.mult).then_inc(rh_ready, 1)
                if not tail:
                    split_matrix(U5)
                for c in range(KC):
                    dve.wait_ge(rh_hi_ready, 2 * s + c + 1)
                    nc.vector.tensor_tensor(rh_lo[:, c, :], rh[:, c, :], bits(rh_hi[:, c, :]),
                                            ALU.subtract).then_inc(rh_split, 1)
                if not tail:
                    split_new(1, 1)
                if j in (2, 3) and more:
                    measure(2 * (pair + 1) + q, pair + 1, q)
                if j == SEGS - 2 and more:
                    make_new_blocks(2 * (pair + 1), q)
                if tail and not last_step:
                    take_state(s - 1, 1 - q, moved_before(pair, j + 1))
                elif tail:
                    add_x(pair if j else pair - 1, 1 - q, s - 1)
                if new:
                    take_new(1 - q, s + 1, new_group(pair, j))
                if j == SEGS - 1 and more:
                    make_new_blocks(2 * (pair + 1) + 1, q)

            def sum_halves(k):
                dve.wait_ge(loaded[k], 16)
                nc.vector.tensor_tensor(w_sum[k][:], w_nat[k][:, :, 0:D], w_nat[k][:, :, D:2 * D],
                                        ALU.add).then_inc(w_summed, 1)

            measure(0, 0, 0, first=True)
            normalise(0, 0)
            split_matrix(ADJ)
            sum_halves("w4")
            split_new(0, 0)
            dve.wait_ge(bias_turned, 1)
            nc.vector.tensor_copy(bias_cols[:], ps_h[:, 1, 0:5 * KC]).then_inc(bias_copied, 1)
            dve.wait_ge(bias_copied, 1)
            b_w3, b_u3, b_w4, b_w5, b_u5 = (bias_cols[:, i * KC:(i + 1) * KC] for i in range(5))
            nc.vector.tensor_tensor(bias_z[:], b_w3, b_u3, ALU.add).then_inc(bias_ready, 1)
            nc.vector.tensor_tensor(bias_r[:], b_w4, b_u3, ALU.add).then_inc(bias_ready, 1)
            nc.vector.tensor_tensor(bias_h[:], b_w5, b_u5, ALU.add).then_inc(bias_ready, 1)
            split_matrix(U3)
            sum_halves("w5")
            take_new(0, 0, 0)
            sum_halves("w3")
            split_matrix(W4)
            dve.wait_ge(w_summed, 3)
            nc.vector.tensor_tensor(w_diff[:], w_sum["w3"][:], w_sum["w4"][:], ALU.subtract).then_inc(w_summed, 1)

            segment(0, 0, tail=False, new=True)
            with dve.Fori(0, PAIRS - 1) as pair:
                for j in range(1, SEGS):
                    segment(pair, j, new=j == SEGS - 1)
                segment(pair + 1, 0, new=True)
            for j in range(1, SEGS):
                segment(PAIRS - 1, j, more=False)
            make_delta(LAST, 1, 0)
            make_zdelta(LAST, 0)
            make_delta(LAST, 1, 1)
            make_state(LAST, 1, 0)
            make_zdelta(LAST, 1)
            make_state(LAST, 1, 1)
            add_x_last()


_INS = ["x", "adj", "L0_gnn_w3_w", "L0_gnn_w3_b", "L0_gnn_u3_w", "L0_gnn_u3_b", "L0_gnn_w4_w", "L0_gnn_w4_b",
        "L0_gnn_w5_w", "L0_gnn_w5_b", "L0_gnn_u5_w", "L0_gnn_u5_b"]


def kernel(**inputs):
    import numpy as _np
    import concourse.bacc as _bacc
    from concourse import mybir as _mybir
    from concourse.bass_utils import run_bass_kernel_spmd as _run

    nc = _bacc.Bacc("TRN2", target_bir_lowering=False, num_devices=1)
    arrays, args = {}, []
    for name in _INS:
        a = _np.ascontiguousarray(inputs[name])
        arrays[f"in_{name}"] = a
        args.append(nc.dram_tensor(f"in_{name}", a.shape, _mybir.dt.from_np(a.dtype), kind="ExternalInput").ap())
    x = inputs["x"]
    args.append(nc.dram_tensor("out_x", x.shape, _mybir.dt.from_np(_np.dtype("float32")), kind="ExternalOutput").ap())
    gnn_kernel(nc, *args)
    r = _run(nc, [arrays], core_ids=[0])
    return r.results[0]["out_x"]
```
